# Optimizing a Trainium2 kernel written in Bass

```python
import numpy as np
import jax
import jax.numpy as jnp

def _softmax(x, axis=-1):
    return jax.nn.softmax(x, axis=axis)

def _gelu(x):
    return jax.nn.gelu(x, approximate=True)

def _silu(x):
    return jax.nn.silu(x)

def _sigmoid(x):
    return jax.nn.sigmoid(x)

def _layernorm(x, axis=-1, eps=1e-05):
    m = jnp.mean(x, axis=axis, keepdims=True)
    v = jnp.var(x, axis=axis, keepdims=True)
    return (x - m) / jnp.sqrt(v + eps)

def _scatter_add(tgt, idx, src, axis=0):
    return tgt.at[idx].add(src)

def _segment_sum(src, seg, n):
    return jax.ops.segment_sum(src, seg, n)
kernel_name = 'mk_gnn_preln_d2_gnn_r8_fe1c5e'

def setup_inputs(seed: int=0):
    np.random.seed(seed)
    _w = jnp.asarray

    def _rec_inputs():
        import jax
        import jax.numpy as jnp
        _gk = jax.random.key(seed)
        x = -0.0003713 + 1 * jax.random.normal(jax.random.fold_in(_gk, 1), (6250, 128), jnp.float32)
        _s = jax.random.randint(jax.random.fold_in(_gk, 2), (100000,), 0, 6250, jnp.int32)
        _d = jax.random.randint(jax.random.fold_in(_gk, 3), (100000,), 0, 6250, jnp.int32)
        _loop = jnp.arange(6250, dtype=jnp.int32)
        src = jnp.concatenate([_s, _d, _loop])
        dst = jnp.concatenate([_d, _s, _loop])
        _o = jnp.argsort(dst, stable=True)
        src = src[_o]
        dst = dst[_o]
        edge_attr_128 = 9.41057e-06 + 1 * jax.random.normal(jax.random.fold_in(_gk, 13), (206250, 128), jnp.float32)
        return (x, src, dst, edge_attr_128)
    x, src, dst, edge_attr_128 = _rec_inputs()

    def _L0_gnn_setup():
        import jax, jax.numpy as jnp
        import numpy as np
        N_NODES = 12500
        N_EDGES = 200000
        D_IN = 128
        D_OUT = 128
        BN_EPS = 1e-05
        key = jax.random.key(seed)
        ks = jax.random.split(key, 6)
        X = jax.random.normal(ks[0], (N_NODES, D_IN), dtype=jnp.float32)
        W = jax.random.normal(ks[1], (D_OUT, D_IN), dtype=jnp.float32) * (1.0 / np.sqrt(D_IN))
        b = jax.random.normal(ks[2], (D_OUT,), dtype=jnp.float32) * 0.01
        gamma = jnp.ones((D_OUT,), dtype=jnp.float32)
        beta = jnp.zeros((D_OUT,), dtype=jnp.float32)
        src = jax.random.randint(ks[3], (N_EDGES,), 0, N_NODES, dtype=jnp.int64 if jax.config.read('jax_enable_x64') else jnp.int32)
        dst = jax.random.randint(ks[4], (N_EDGES,), 0, N_NODES, dtype=jnp.int64 if jax.config.read('jax_enable_x64') else jnp.int32)
        return {'X': X, 'W': W, 'b': b, 'gamma': gamma, 'beta': beta, 'src': src, 'dst': dst}
    _L0_gnn_all = _L0_gnn_setup()
    _L0_gnn_in = {k: v for k, v in _L0_gnn_all.items() if k in ('W', 'b', 'gamma', 'beta')}
    del _L0_gnn_all

    def _L1_gnn_setup():
        import jax, jax.numpy as jnp
        import numpy as np
        N_NODES = 12500
        N_EDGES = 200000
        N_GRAPHS = 64
        D_X = 128
        D_E = 128
        D_U = 128
        HIDDEN = 128
        OUT = 128
        IN_SIZE = D_X + D_E + D_U
        key = jax.random.key(seed)
        ks = jax.random.split(key, 10)
        x = jax.random.normal(ks[0], (N_NODES, D_X), dtype=jnp.float32)
        edge_index = jax.random.randint(ks[1], (2, N_EDGES), 0, N_NODES, dtype=jnp.int64)
        edge_attr = jax.random.normal(ks[2], (N_EDGES, D_E), dtype=jnp.float32)
        u = jax.random.normal(ks[3], (N_GRAPHS, D_U), dtype=jnp.float32)
        batch = jnp.sort(jax.random.randint(ks[4], (N_NODES,), 0, N_GRAPHS, dtype=jnp.int64))
        W1 = jax.random.normal(ks[5], (IN_SIZE, HIDDEN), dtype=jnp.float32) * (1.0 / np.sqrt(IN_SIZE))
        b1 = jnp.zeros((HIDDEN,), dtype=jnp.float32)
        W2 = jax.random.normal(ks[6], (HIDDEN, HIDDEN), dtype=jnp.float32) * (1.0 / np.sqrt(HIDDEN))
        b2 = jnp.zeros((HIDDEN,), dtype=jnp.float32)
        W3 = jax.random.normal(ks[7], (HIDDEN, OUT), dtype=jnp.float32) * (1.0 / np.sqrt(HIDDEN))
        b3 = jnp.zeros((OUT,), dtype=jnp.float32)
        return {'x': x, 'edge_index': edge_index, 'edge_attr': edge_attr, 'u': u, 'batch': batch, 'W1': W1, 'b1': b1, 'W2': W2, 'b2': b2, 'W3': W3, 'b3': b3}
    _L1_gnn_all = _L1_gnn_setup()
    _L1_gnn_in = {k: v for k, v in _L1_gnn_all.items() if k in ('u', 'W1', 'b1', 'W2', 'b2', 'W3', 'b3')}
    del _L1_gnn_all
    return {'x': x, 'src': src, 'dst': dst, 'edge_attr_128': edge_attr_128, 'L0_gnn_W': _L0_gnn_in['W'], 'L0_gnn_b': _L0_gnn_in['b'], 'L0_gnn_gamma': _L0_gnn_in['gamma'], 'L0_gnn_beta': _L0_gnn_in['beta'], 'L1_gnn_u': _L1_gnn_in['u'], 'L1_gnn_W1': _L1_gnn_in['W1'], 'L1_gnn_b1': _L1_gnn_in['b1'], 'L1_gnn_W2': _L1_gnn_in['W2'], 'L1_gnn_b2': _L1_gnn_in['b2'], 'L1_gnn_W3': _L1_gnn_in['W3'], 'L1_gnn_b3': _L1_gnn_in['b3']}

def reference(x, src, dst, edge_attr_128, L0_gnn_W, L0_gnn_b, L0_gnn_gamma, L0_gnn_beta, L1_gnn_u, L1_gnn_W1, L1_gnn_b1, L1_gnn_W2, L1_gnn_b2, L1_gnn_W3, L1_gnn_b3):
    import jax
    import jax.numpy as jnp

    def _L0_gnn_ref(X, W, b, gamma, beta, src, dst):
        import jax, jax.numpy as jnp
        import numpy as np
        N_NODES = 12500
        N_EDGES = 200000
        D_IN = 128
        D_OUT = 128
        BN_EPS = 1e-05
        H = X @ W.T + b
        mu = jnp.mean(H, axis=0)
        var = jnp.mean(jnp.square(H - mu), axis=0)
        H = (H - mu) * jax.lax.rsqrt(var + BN_EPS) * gamma + beta
        n = X.shape[0]
        ones = jnp.ones(dst.shape, dtype=H.dtype)
        deg_hat = 1.0 + jax.ops.segment_sum(ones, dst, num_segments=n)
        dinv = jax.lax.rsqrt(deg_hat)
        norm = dinv[src] * dinv[dst]
        msg = H[src] * norm[:, None]
        out = jax.ops.segment_sum(msg, dst, num_segments=n)
        out = out + H * (dinv * dinv)[:, None]
        return jax.nn.relu(out)

    def _L1_gnn_ref(x, edge_index, edge_attr, u, batch, W1, b1, W2, b2, W3, b3):
        import jax, jax.numpy as jnp
        import numpy as np
        N_NODES = 12500
        N_EDGES = 200000
        N_GRAPHS = 64
        D_X = 128
        D_E = 128
        D_U = 128
        HIDDEN = 128
        OUT = 128
        IN_SIZE = D_X + D_E + D_U
        edge_dst = edge_index[1]
        agg = jax.ops.segment_sum(edge_attr, edge_dst, num_segments=x.shape[0])
        model_in = jnp.concatenate([x, agg, u[batch]], axis=1)
        h = jax.nn.relu(model_in @ W1 + b1)
        h = jax.nn.relu(h @ W2 + b2)
        return h @ W3 + b3
    edge_index = jnp.stack([src, dst])
    batch0 = jnp.zeros((6250,), jnp.int32)
    h = jnp.maximum(_layernorm(x, axis=-1), 0.0)
    x = x + _L0_gnn_ref(h, L0_gnn_W, L0_gnn_b, L0_gnn_gamma, L0_gnn_beta, src, dst)
    h = jnp.maximum(_layernorm(x, axis=-1), 0.0)
    x = x + _L1_gnn_ref(h, edge_index, edge_attr_128, L1_gnn_u, batch0, L1_gnn_W1, L1_gnn_b1, L1_gnn_W2, L1_gnn_b2, L1_gnn_W3, L1_gnn_b3)
    return x

_drawn_inputs = setup_inputs


def setup_inputs(seed=0):
    import zlib

    import numpy as np

    out = dict(_drawn_inputs(seed))
    spreads = {'L0_gnn_gamma': (1.0, 0.6),
     'L0_gnn_beta': (0.0, 0.1),
     'L1_gnn_b1': (0.0, 0.345),
     'L1_gnn_b2': (0.0, 0.1),
     'L1_gnn_b3': (0.0, 0.1)}
    factors = {'L0_gnn_b': 8.0}
    for name, (base, spread) in spreads.items():
        noise = np.random.default_rng([zlib.crc32(name.encode()), seed]).standard_normal(out[name].shape)
        drawn = base * np.exp(spread * noise) if base else spread * noise
        out[name] = jnp.asarray(drawn.astype(out[name].dtype))
    for name, factor in factors.items():
        out[name] = (out[name] * factor).astype(out[name].dtype)
    return out
```

```python
from contextlib import ExitStack

import concourse.bass as bass
from concourse import mybir

F32 = mybir.dt.float32
BF16 = mybir.dt.bfloat16
I32 = mybir.dt.int32
ALU = mybir.AluOpType
ACT = mybir.ActivationFunctionType
AX = mybir.AxisListType

P = 128
TILE = 128
GT = 4
W = 32
UN = 4
EPS = 1e-5
NOWHERE = 1.0e6


def gnn_kernel(nc, x, src, dst, edge_attr, w_gcn, b_gcn, gamma, beta, u, w1, b1, w2, b2, w3, b3, out):
    N, D = x.shape
    E = src.shape[0]
    assert D == P
    NC = 512
    BC = NC // P
    CHUNKS = -(-N // NC)
    NB = CHUNKS * BC
    NPAD = CHUNKS * NC
    FB = N // P
    TAILN = N - FB * P
    GE = GT * TILE
    FULL = E // GE
    OVER = (FULL + 1) * GE - E
    NG = -(-(FULL + 1) // UN) * UN
    NU = NG // UN
    RC = -(-NG // P)
    AW = NPAD + W
    BNC = 250
    assert N % BNC == 0 and E % GE and TAILN > 96 and FB == NB - BC

    table = nc.dram_tensor("scaled_h_table", (NPAD, P), F32, kind="Internal").ap()
    src_rows = src[0:FULL * GE].rearrange("(g e) -> g e", e=GE)
    dst_rows = dst[0:FULL * GE].rearrange("(g e) -> g e", e=GE)
    src_last = src[E - GE:E].rearrange("(a e) -> a e", a=1)
    dst_last = dst[E - GE:E].rearrange("(a e) -> a e", a=1)
    attr_groups = edge_attr[0:FULL * GE, :].rearrange("(g p t) f -> g p (t f)", p=P, t=GT)
    attr_last = edge_attr[E - GE:E, :].rearrange("(p t) f -> p (t f)", t=GT)
    x_full = x[0:FB * P, :].rearrange("(b p) f -> p b f", p=P)
    table_blocks = table.rearrange("(b p) f -> p b f", p=P)
    out_full = out[0:FB * P, :].rearrange("(b p) f -> p b f", p=P)

    with ExitStack() as ctx:
        def sb(name, shape, dt=F32):
            return ctx.enter_context(nc.sbuf_tensor(name, shape, dt))

        def sem(name):
            return ctx.enter_context(nc.semaphore(name))

        def looped(eng, n, step):
            step(0, True)
            with eng.Fori(1, n) as i:
                step(i, False)

        def layer_norm_stats(v, link, var_ready, root_ready, norm_ready):
            m0, m1, s0, s1 = stats[:, :, 1], stats[:, :, 4], stats[:, :, 2], stats[:, :, 5]
            v.tensor_tensor(mean[:], m0, m1, ALU.add)
            v.tensor_tensor(shift[:], m0, m1, ALU.subtract)
            link(v.tensor_tensor(rstd[:], s0, s1, ALU.add))
            v.tensor_scalar(mean[:], mean[:], 0.5, None, ALU.mult)
            link(v.scalar_tensor_tensor(out=shift[:], in0=shift[:], scalar=0.25, in1=shift[:],
                                        op0=ALU.mult, op1=ALU.mult))
            v.scalar_tensor_tensor(out=var[:], in0=rstd[:], scalar=1.0 / P, in1=shift[:],
                                   op0=ALU.mult, op1=ALU.add).then_inc(var_ready, 1)
            v.wait_ge(root_ready, 1)
            link(v.reciprocal(rstd[:], rstd[:]))
            v.scalar_tensor_tensor(out=shift[:], in0=mean[:], scalar=-1.0, in1=rstd[:],
                                   op0=ALU.mult, op1=ALU.mult).then_inc(norm_ready, 1)

        xs = sb("xs", [P, NB, P])
        stats = sb("stats", [P, NB, 6])
        var = sb("var", [P, NB])
        mean = sb("mean", [P, NB])
        rstd = sb("rstd", [P, NB])
        shift = sb("shift", [P, NB])
        h_t = sb("h_t", [P, NPAD])
        acc = sb("acc", [P, 2, AW])
        dinv = sb("dinv", [P, AW])
        dst_t = sb("dst_t", [P, NG, GT])
        rel_t = sb("rel_t", [P, NG, GT])
        src_t = sb("src_t", [P, NG, GT])
        base_row = sb("base_row", [1, NG])
        window_row = sb("window_row", [1, NG])
        window_int = sb("window_int", [1, NG], I32)
        span_int = sb("span_int", [1, 1], I32)
        iota_w = sb("iota_w", [P, W])
        ident = sb("ident", [P, P])
        ones_row = sb("ones_row", [1, P])
        ones_bf = sb("ones_bf", [P, P], BF16)
        eps_col = sb("eps_col", [P, 1])
        wg_t = sb("wg_t", [P, P])
        w1_sb = sb("w1_sb", [P, 3, P])
        w2_sb = sb("w2_sb", [P, P])
        w3_sb = sb("w3_sb", [P, P])
        b3_row = sb("b3_row", [1, P])
        cols = sb("cols", [P, 8])
        B_GCN, GAMMA, BETA, B1, B2, U = (cols[:, k:k + 1] for k in range(6))
        b1u = sb("b1u", [P, 1])
        bn = sb("bn", [P, 8])

        with ExitStack() as scope:
            def sb1(name, shape, dt=F32):
                return scope.enter_context(nc.sbuf_tensor(name, shape, dt))

            def ps1(name, shape):
                return scope.enter_context(nc.psum_tensor(name, shape, F32))

            def sem1(name):
                return scope.enter_context(nc.semaphore(name))

            raw = sb1("raw", [P, RC, GE], I32)
            raw_last = sb1("raw_last", [1, GE], I32)
            edge_f = sb1("edge_f", [P, RC, GE])
            last_f = sb1("last_f", [1, GE])
            lim = sb1("lim", [P, 2, RC])
            spans = sb1("spans", [P, 2])
            unmasked = sb1("unmasked", [P, RC, GE])
            w_raw = sb1("w_raw", [P, P])
            h_ring = sb1("h_ring", [P, 2, BC, P])
            ht_ring = sb1("ht_ring", [P, 2, NC])
            bstats = sb1("bstats", [P, N // BNC, 6])
            turn = [ps1(f"turn{k}", [P, GT, P]) for k in range(2)]
            ps_turn = [ps1(f"ps_turn{k}", [P, BC, P]) for k in range(2)]
            ps_lin = [ps1(f"ps_lin{k}", [P, NC]) for k in range(2)]
            ps_small = ps1("ps_small", [P, 512])

            x_in, dst_in, src_in, last_in, w_in = (sem1(n) for n in ("x_in", "dst_in", "src_in", "last_in", "w_in"))
            dst_cast, src_cast, last_put = (sem1(n) for n in ("dst_cast", "src_cast", "last_put"))
            zeroed, ident_ok, consts = (sem1(n) for n in ("zeroed", "ident_ok", "consts"))
            turned, turn_read, src_read = (sem1(n) for n in ("turned", "turn_read", "src_read"))
            limits, span_t = (sem1(n) for n in ("limits", "span_t"))
            dve_step, var_ok, root_ok, norm_ok = (sem1(n) for n in ("dve_step", "var_ok", "root_ok", "norm_ok"))
            h_ready, h_turned, ht_ready = (sem1(n) for n in ("h_ready", "h_turned", "ht_ready"))
            lin_ready, lin_saved = (sem1(n) for n in ("lin_ready", "lin_saved"))
            w_turned, wg_ready, b1u_done = (sem1(n) for n in ("w_turned", "wg_ready", "b1u_done"))
            bvar_ok, broot_ok = (sem1(n) for n in ("bvar_ok", "broot_ok"))
            W_LOADS = 11

            def rows(c):
                return min(P, FULL + 1 - c * P)

            with nc.Block() as block:
                @block.sync
                def _(sp):
                    last = FULL - (RC - 1) * P

                    def load_rows(view, arrived):
                        for c in range(RC):
                            n = min(P, FULL - c * P)
                            sp.dma_start(raw[0:n, c, :], view[c * P:c * P + n, :]).then_inc(arrived, 16)

                    load_rows(dst_rows, dst_in)
                    sp.dma_start(raw_last[:], dst_last).then_inc(last_in, 16)
                    sp.dma_start(xs[:, 0:FB, :], x_full).then_inc(x_in, 16)
                    sp.wait_ge(zeroed, 1)
                    sp.dma_start(xs[0:TAILN, FB, :], x[FB * P:N, :]).then_inc(x_in, 16)
                    sp.dma_start(w_raw[:], w_gcn).then_inc(w_in, 16)
                    for k, vec in enumerate((b_gcn, gamma, beta, b1, b2)):
                        sp.dma_start(cols[:, k:k + 1], vec.rearrange("(p a) -> p a", a=1)).then_inc(w_in, 16)
                    sp.dma_start(U, u[0:1, :].rearrange("a p -> p a")).then_inc(w_in, 16)
                    sp.dma_start(w1_sb[:], w1.rearrange("(k p) n -> p k n", p=P)).then_inc(w_in, 16)
                    sp.dma_start(w2_sb[:], w2).then_inc(w_in, 16)
                    sp.dma_start(w3_sb[:], w3).then_inc(w_in, 16)
                    sp.dma_start(b3_row[:], b3.rearrange("(a n) -> a n", a=1)).then_inc(w_in, 16)
                    sp.wait_ge(dst_cast, 2)
                    sp.dma_start(edge_f[last:last + 1, RC - 1, :], last_f[:]).then_inc(last_put, 16)
                    load_rows(src_rows, src_in)
                    sp.dma_start(raw[last:last + 1, RC - 1, :], src_last).then_inc(src_in, 16)
                    sp.wait_ge(last_put, 16)
                    sp.wait_ge(src_in, 16 * (RC + 1))

                @block.gpsimd
                def _(pool):
                    pool.memset(xs[:, FB:NB, :], 0.0).then_inc(zeroed, 1)
                    pool.memset(ident[:], 0.0).then_inc(consts, 1)
                    pool.wait_ge(consts, 1)
                    pool.affine_select(out=ident[:], in_=ident[:], compare_op=ALU.not_equal, fill=1.0, base=0,
                                       pattern=[[-1, P]], channel_multiplier=1).then_inc(ident_ok, 1)
                    pool.iota(iota_w[:], [[1, W]], base=0, channel_multiplier=0,
                              allow_small_or_imprecise_dtypes=True).then_inc(consts, 1)
                    pool.memset(ones_row[:], 1.0).then_inc(consts, 1)
                    pool.memset(ones_bf[:], 1.0).then_inc(consts, 1)
                    pool.memset(dinv[:], 0.0).then_inc(consts, 1)
                    pool.memset(acc[:], 0.0).then_inc(consts, 1)
                    pool.wait_ge(consts, 6)

                @block.vector
                def _(v):
                    chain = [0]

                    def link(ins):
                        chain[0] += 1
                        ins.then_inc(dve_step, 1)
                        v.wait_ge(dve_step, chain[0])

                    v.memset(lim[:], 0.0)
                    v.memset(base_row[:], 0.0)
                    v.memset(spans[:], 0.0)
                    v.memset(dst_t[:], NOWHERE)
                    v.memset(src_t[:], 0.0)
                    link(v.memset(eps_col[:], EPS))
                    v.wait_ge(last_in, 16)
                    link(v.tensor_copy(last_f[:], raw_last[:]))
                    v.memset(last_f[:, 0:OVER], NOWHERE).then_inc(dst_cast, 1)
                    v.wait_ge(dst_in, 16 * RC)
                    for c in range(RC):
                        n = min(P, FULL - c * P)
                        ins = v.tensor_copy(edge_f[0:n, c, :], raw[0:n, c, :])
                    ins.then_inc(dst_cast, 1)
                    v.wait_ge(dst_cast, 2)
                    v.wait_ge(last_put, 16)
                    for c in range(RC):
                        r = rows(c)
                        v.tensor_reduce(lim[0:r, 0, c:c + 1], edge_f[0:r, c, :], AX.X, ALU.min)
                        ins = v.scalar_tensor_tensor(out=unmasked[0:r, c, :], in0=edge_f[0:r, c, :],
                                                     scalar=NOWHERE / 2, in1=edge_f[0:r, c, :],
                                                     op0=ALU.is_lt, op1=ALU.mult)
                    link(ins)
                    for c in range(RC):
                        r = rows(c)
                        ins = v.tensor_reduce(lim[0:r, 1, c:c + 1], unmasked[0:r, c, :], AX.X, ALU.max)
                    link(ins)
                    link(v.tensor_tensor(lim[:, 1, :], lim[:, 1, :], lim[:, 0, :], ALU.subtract))
                    v.tensor_reduce(spans[:, 0:1], lim[:, 1, :], AX.X, ALU.max).then_inc(limits, 1)
                    for c in range(RC):
                        v.wait_ge(turned, c + 1)
                        v.tensor_copy(dst_t[:, c * P:c * P + rows(c), :].rearrange("p g t -> p t g"),
                                      turn[c % 2][:, :, 0:rows(c)]).then_inc(turn_read, 1)
                    v.wait_ge(span_t, 1)
                    for c in range(RC):
                        v.tensor_copy(base_row[:, c * P:c * P + rows(c)], ps_small[0:1, c * P:c * P + rows(c)])
                    link(v.tensor_reduce(spans[0:1, 1:2], ps_lin[0][0:1, 0:P], AX.X, ALU.max))
                    v.tensor_scalar(window_row[:], base_row[:], -float(W), None, ALU.add)
                    v.tensor_copy(span_int[:], spans[0:1, 1:2])
                    v.wait_ge(w_turned, 1)
                    v.tensor_copy(wg_t[:], ps_turn[1][:, 0, :]).then_inc(wg_ready, 1)

                    v.wait_ge(x_in, 32)
                    for b in range(NB):
                        ins = v.bn_stats(stats[:, b, :], xs[:, b, :])
                    link(ins)
                    layer_norm_stats(v, link, var_ok, root_ok, norm_ok)

                    for c in range(CHUNKS):
                        v.wait_ge(h_turned, c + 1)
                        if c >= 2:
                            v.wait_ge(lin_ready, c - 1)
                        v.tensor_copy(ht_ring[:, c % 2, :], ps_turn[c % 2][:].rearrange("p b n -> p (b n)"))\
                         .then_inc(ht_ready, 1)

                    v.wait_ge(lin_saved, CHUNKS)
                    for c in range(N // BNC):
                        ins = v.bn_stats(bstats[:, c, :], h_t[:, c * BNC:(c + 1) * BNC])
                    link(ins)
                    v.bn_aggr(bn[:, 0:2], bstats[:].rearrange("p c s -> p (c s)")).then_inc(bvar_ok, 1)
                    v.wait_ge(broot_ok, 1)
                    link(v.reciprocal(bn[:, 3:4], bn[:, 2:3]))
                    link(v.tensor_tensor(bn[:, 4:5], bn[:, 3:4], GAMMA, ALU.mult))
                    link(v.tensor_tensor(bn[:, 5:6], bn[:, 0:1], bn[:, 4:5], ALU.mult))
                    link(v.tensor_tensor(bn[:, 6:7], BETA, bn[:, 5:6], ALU.subtract))
                    v.tensor_scalar(h_t[:], h_t[:], bn[:, 4:5], bn[:, 6:7], ALU.mult, ALU.add)
                    v.wait_ge(b1u_done, 1)
                    v.tensor_tensor(b1u[:], ps_small[:, 448:449], B1, ALU.add)

                @block.scalar
                def _(act):
                    act.wait_ge(src_in, 16 * (RC + 1))
                    act.wait_ge(turned, RC)
                    act.wait_ge(limits, 1)
                    for c in range(RC):
                        ins = act.copy(edge_f[0:rows(c), c, :], raw[0:rows(c), c, :])
                    ins.then_inc(src_cast, 1)
                    for c in range(RC):
                        act.wait_ge(turned, RC + c + 1)
                        act.copy(src_t[:, c * P:c * P + rows(c), :].rearrange("p g t -> p t g"),
                                 turn[(RC + c) % 2][:, :, 0:rows(c)]).then_inc(src_read, 1)
                    act.wait_ge(var_ok, 1)
                    act.activation(rstd[:], var[:], ACT.Sqrt, bias=eps_col[:]).then_inc(root_ok, 1)
                    act.wait_ge(norm_ok, 1)
                    act.wait_ge(w_in, 16 * W_LOADS)

                    for c in range(CHUNKS + 1):
                        if c < CHUNKS:
                            if c >= 2:
                                act.wait_ge(h_turned, c - 1)
                            for k in range(BC):
                                n = c * BC + k
                                ins = act.activation(h_ring[:, c % 2, k, :], xs[:, n, :], ACT.Relu,
                                                     scale=rstd[:, n:n + 1], bias=shift[:, n:n + 1])
                            ins.then_inc(h_ready, 1)
                        if c >= 1:
                            act.wait_ge(lin_ready, c)
                            act.activation(h_t[:, (c - 1) * NC:c * NC], ps_lin[(c - 1) % 2][:], ACT.Identity,
                                           bias=B_GCN).then_inc(lin_saved, 1)
                    act.wait_ge(bvar_ok, 1)
                    act.activation(bn[:, 2:3], bn[:, 1:2], ACT.Sqrt, bias=eps_col[:]).then_inc(broot_ok, 1)

                @block.tensor
                def _(pe):
                    def turn_rows(t, c):
                        if t >= 2:
                            pe.wait_ge(*((turn_read, t - 1) if t - 2 < RC else (src_read, t - 1 - RC)))
                        r = rows(c)
                        for j in range(GT):
                            ins = pe.transpose(turn[t % 2][:, j, 0:r],
                                               edge_f[0:r, c, :].rearrange("g (p t) -> g t p", t=GT)[:, j, :],
                                               ident[0:r, 0:r])
                        ins.then_inc(turned, 1)

                    pe.wait_ge(ident_ok, 1)
                    pe.wait_ge(dst_cast, 2)
                    pe.wait_ge(last_put, 16)
                    for c in range(RC):
                        turn_rows(c, c)
                    pe.wait_ge(limits, 1)
                    for c in range(RC):
                        pe.transpose(ps_small[0:1, c * P:(c + 1) * P], lim[:, 0, c:c + 1], ident[:])
                    pe.transpose(ps_lin[0][0:1, 0:P], spans[:, 0:1], ident[:]).then_inc(span_t, 1)
                    pe.wait_ge(w_in, 16 * W_LOADS)
                    pe.transpose(ps_turn[1][:, 0, :], w_raw[:], ident[:]).then_inc(w_turned, 1)
                    pe.wait_ge(src_cast, 1)
                    for c in range(RC):
                        turn_rows(RC + c, c)
                    pe.wait_ge(wg_ready, 1)

                    for c in range(CHUNKS + 1):
                        if c < CHUNKS:
                            pe.wait_ge(h_ready, c + 1)
                            if c >= 2:
                                pe.wait_ge(ht_ready, c - 1)
                            for k in range(BC):
                                ins = pe.transpose(ps_turn[c % 2][:, k, :], h_ring[:, c % 2, k, :], ident[:])
                            ins.then_inc(h_turned, 1)
                        if c >= 1:
                            pe.wait_ge(ht_ready, c)
                            if c >= 3:
                                pe.wait_ge(lin_saved, c - 2)
                            pe.matmul(ps_lin[(c - 1) % 2][:], wg_t[:], ht_ring[:, (c - 1) % 2, :], start=True,
                                      stop=True).then_inc(lin_ready, 1)
                    pe.matmul(ps_small[:, 448:449], w1_sb[:, 2, :], U, start=True, stop=True).then_inc(b1u_done, 1)

        span = nc.values_load(span_int[0:1, 0:1], min_val=0, max_val=N - 1)
        passes = nc.snap(span // W + 1)

        def move_windows(tag, stale):
            with ExitStack() as scope:
                starts = scope.enter_context(nc.psum_tensor(f"{tag}_starts", [P, 512], F32))
                moved = scope.enter_context(nc.semaphore(f"{tag}_moved"))
                spread = scope.enter_context(nc.semaphore(f"{tag}_spread"))
                with nc.Block() as block:
                    @block.vector
                    def _(v):
                        for s in stale:
                            v.sem_clear(s)
                        v.tensor_scalar(window_row[:], window_row[:], float(W), float(NPAD), ALU.add,
                                        ALU.min).then_inc(moved, 1)
                        v.wait_ge(moved, 1)
                        v.tensor_copy(window_int[:], window_row[:])
                        v.wait_ge(spread, 1)
                        v.tensor_tensor(rel_t[:], dst_t[:], starts[:, 0:NG].unsqueeze(2).to_broadcast([P, NG, GT]),
                                        ALU.subtract)

                    @block.tensor
                    def _(pe):
                        pe.wait_ge(moved, 1)
                        pe.matmul(starts[:, 0:NG], ones_row[:], window_row[:], start=True, stop=True)\
                          .then_inc(spread, 1)
                with nc.Block() as block:
                    @block.vector
                    def _(v):
                        v.sem_clear(moved)
                        v.sem_clear(spread)

        def one_hot(v, target, g):
            rel = rel_t[:, bass.ds(g, 1), :].rearrange("p a t -> p (a t)")
            return v.tensor_tensor(target, rel.unsqueeze(2).to_broadcast([P, GT, W]),
                                   iota_w[:].unsqueeze(1).to_broadcast([P, GT, W]), ALU.is_equal)

        with ExitStack() as scope:
            onehot = scope.enter_context(nc.sbuf_tensor("deg_onehot", [P, UN, GT, W], BF16))
            counts = [scope.enter_context(nc.psum_tensor(f"counts{k}", [P, 512], F32)) for k in range(UN)]
            hot_ready = scope.enter_context(nc.semaphore("deg_hot_ready"))
            counted = scope.enter_context(nc.semaphore("deg_counted"))
            added = scope.enter_context(nc.semaphore("deg_added"))
            with nc.Fori(0, passes):
                move_windows("deg", (hot_ready, counted, added))
                with nc.Block() as block:
                    @block.vector
                    def _(v):
                        regs = [v.alloc_register(f"deg_start{k}") for k in range(UN)]

                        def step(i, first):
                            v.load(regs, window_int[0:1, bass.ds(i * UN, UN)])
                            for k in range(UN):
                                if not first:
                                    v.wait_ge(counted, i * UN + k + 1 - UN)
                                one_hot(v, onehot[:, k, :, :], i * UN + k).then_inc(hot_ready, 1)
                            for k in range(UN):
                                start = v.snap(regs[k], min_val=0, max_val=NPAD)
                                v.wait_ge(counted, i * UN + k + 1)
                                if not (first and k == 0):
                                    v.wait_ge(added, i * UN + k)
                                win = dinv[:, bass.ds(start, W)]
                                v.tensor_tensor(win, win, counts[k][:, 0:W], ALU.add).then_inc(added, 1)
                        looped(v, NU, step)

                    @block.tensor
                    def _(pe):
                        def step(i, first):
                            for k in range(UN):
                                pe.wait_ge(hot_ready, i * UN + k + 1)
                                if not first:
                                    pe.wait_ge(added, i * UN + k + 1 - UN)
                                for t in range(GT):
                                    ins = pe.matmul(counts[k][:, 0:W], ones_bf[:], onehot[:, k, t, :],
                                                    start=(t == 0), stop=(t == GT - 1))
                                ins.then_inc(counted, 1)
                        looped(pe, NU, step)

        with ExitStack() as scope:
            hs_ring = scope.enter_context(nc.sbuf_tensor("hs_ring", [P, 2, NC], F32))
            row_ring = scope.enter_context(nc.sbuf_tensor("row_ring", [P, 2, BC, P], F32))
            ps_rows = [scope.enter_context(nc.psum_tensor(f"ps_rows{k}", [P, BC, P], F32)) for k in range(2)]
            deg_root = scope.enter_context(nc.semaphore("deg_root"))
            dinv_ok = scope.enter_context(nc.semaphore("dinv_ok"))
            hs_ready = scope.enter_context(nc.semaphore("hs_ready"))
            hs_turned = scope.enter_context(nc.semaphore("hs_turned"))
            row_ready = scope.enter_context(nc.semaphore("row_ready"))
            row_out = [scope.enter_context(nc.semaphore(f"row_out{k}")) for k in range(2)]
            with nc.Block() as block:
                @block.scalar
                def _(act):
                    act.activation(dinv[:], dinv[:], ACT.Sqrt, bias=1.0).then_inc(deg_root, 1)
                    for c in range(CHUNKS):
                        if c >= 2:
                            act.wait_ge(row_out[c % 2], 16 * (c // 2))
                        act.wait_ge(hs_turned, c + 1)
                        act.copy(row_ring[:, c % 2, :, :], ps_rows[c % 2][:]).then_inc(row_ready, 1)

                @block.vector
                def _(v):
                    v.tensor_scalar(window_row[:], base_row[:], -float(W), None, ALU.add)
                    v.wait_ge(deg_root, 1)
                    v.reciprocal(dinv[:], dinv[:]).then_inc(dinv_ok, 1)
                    v.wait_ge(dinv_ok, 1)
                    for c in range(CHUNKS):
                        if c >= 2:
                            v.wait_ge(hs_turned, c - 1)
                        n = slice(c * NC, (c + 1) * NC)
                        v.tensor_tensor(hs_ring[:, c % 2, :], h_t[:, n], dinv[:, n], ALU.mult).then_inc(hs_ready, 1)

                @block.tensor
                def _(pe):
                    for c in range(CHUNKS):
                        pe.wait_ge(hs_ready, c + 1)
                        if c >= 2:
                            pe.wait_ge(row_ready, c - 1)
                        for k in range(BC):
                            ins = pe.transpose(ps_rows[c % 2][:, k, :], hs_ring[:, c % 2, k * P:(k + 1) * P], ident[:])
                        ins.then_inc(hs_turned, 1)

                @block.sync
                def _(sp):
                    for c in range(CHUNKS):
                        sp.wait_ge(row_ready, c + 1)
                        sp.dma_start(table_blocks[:, c * BC:(c + 1) * BC, :], row_ring[:, c % 2, :, :])\
                          .then_inc(row_out[c % 2], 16)
                    for k in range(2):
                        sp.wait_ge(row_out[k], 16 * ((CHUNKS - k + 1) // 2))

        with ExitStack() as scope:
            onehot = scope.enter_context(nc.sbuf_tensor("onehot", [P, UN, GT, W], F32))
            gathered = scope.enter_context(nc.sbuf_tensor("gathered", [P, UN, GT, P], F32))
            attr = scope.enter_context(nc.sbuf_tensor("attr", [P, UN, GT * P], F32))
            index = scope.enter_context(nc.sbuf_tensor("index", [P, UN, GT], I32))
            sums = [scope.enter_context(nc.psum_tensor(f"sums{k}", [P, 512], F32)) for k in range(UN)]
            attr_in = [scope.enter_context(nc.semaphore(f"attr_in{k}")) for k in range(UN)]
            gather_in = [scope.enter_context(nc.semaphore(f"gather_in{k}")) for k in range(UN)]
            index_ready = scope.enter_context(nc.semaphore("index_ready"))
            gathers_open = scope.enter_context(nc.semaphore("gathers_open"))
            hot_ready = scope.enter_context(nc.semaphore("hot_ready"))
            summed = scope.enter_context(nc.semaphore("summed"))
            added = scope.enter_context(nc.semaphore("added"))
            with nc.Fori(0, passes):
                move_windows("edge", (*attr_in, *gather_in, index_ready, gathers_open, hot_ready, summed, added))
                with nc.Block() as block:
                    @block.sync
                    def _(sp):
                        def load(g, k, view):
                            sp.dma_start(attr[:, k, :], view).then_inc(attr_in[k], 16)

                        for k in range(UN):
                            load(k, k, attr_groups[k, :, :])
                        with sp.Fori(1, NU - 1) as i:
                            for k in range(UN):
                                sp.wait_ge(summed, i * UN + k + 1 - UN)
                                load(i, k, attr_groups[bass.ds(i * UN + k, 1), :, :].rearrange("a p n -> p (a n)"))
                        for k in range(UN):
                            g = (NU - 1) * UN + k
                            sp.wait_ge(summed, g + 1 - UN)
                            load(g, k, attr_groups[g, :, :] if g < FULL else attr_last)

                    @block.scalar
                    def _(act):
                        def step(i, first):
                            for k in range(UN):
                                if not first:
                                    act.wait_ge(gather_in[k], 16 * GT * i)
                                act.copy(index[:, k, :], src_t[:, bass.ds(i * UN + k, 1), :]
                                         .rearrange("p a t -> p (a t)")).then_inc(index_ready, 1)
                        looped(act, NU, step)

                    @block.gpsimd
                    def _(pool):
                        def step(i, first):
                            for k in range(UN):
                                pool.wait_ge(index_ready, i * UN + k + 1)
                                if not first:
                                    pool.wait_ge(summed, i * UN + k + 1 - UN)
                                pool.sem_inc(gathers_open, 1)
                                for t in range(GT):
                                    pool.indirect_dma_start(
                                        gathered[:, k, t, :], None, table,
                                        bass.IndirectOffsetOnAxis(ap=index[:, k, t:t + 1], axis=0),
                                    ).then_inc(gather_in[k], 16)
                        looped(pool, NU, step)

                    @block.vector
                    def _(v):
                        regs = [v.alloc_register(f"start{k}") for k in range(UN)]

                        def step(i, first):
                            v.load(regs, window_int[0:1, bass.ds(i * UN, UN)])
                            for k in range(UN):
                                if not first:
                                    v.wait_ge(summed, i * UN + k + 1 - UN)
                                one_hot(v, onehot[:, k, :, :], i * UN + k).then_inc(hot_ready, 1)
                            for k in range(UN):
                                start = v.snap(regs[k], min_val=0, max_val=NPAD)
                                v.wait_ge(summed, i * UN + k + 1)
                                if not (first and k == 0):
                                    v.wait_ge(added, i * UN + k)
                                win = acc[:, :, bass.ds(start, W)]
                                v.tensor_tensor(win, win, sums[k][:, 0:2 * W].rearrange("p (a n) -> p a n", a=2),
                                                ALU.add).then_inc(added, 1)
                        looped(v, NU, step)

                    @block.tensor
                    def _(pe):
                        def step(i, first):
                            for k in range(UN):
                                pe.wait_ge(hot_ready, i * UN + k + 1)
                                if not first:
                                    pe.wait_ge(added, i * UN + k + 1 - UN)
                                pe.wait_ge(attr_in[k], 16 * (i + 1))
                                for t in range(GT):
                                    pe.matmul(sums[k][:, W:2 * W], attr[:, k, t * P:(t + 1) * P], onehot[:, k, t, :],
                                              start=(t == 0), stop=(t == GT - 1))
                                pe.wait_ge(gather_in[k], 16 * GT * (i + 1))
                                for t in range(GT):
                                    ins = pe.matmul(sums[k][:, 0:W], gathered[:, k, t, :], onehot[:, k, t, :],
                                                    start=(t == 0), stop=(t == GT - 1))
                                ins.then_inc(summed, 1)
                        looped(pe, NU, step)

        with ExitStack() as scope:
            def sb5(name):
                return scope.enter_context(nc.sbuf_tensor(name, [P, 2, NC], F32))

            def sem5(name):
                return scope.enter_context(nc.semaphore(name))

            out_ring, h2_ring, h2t_ring, z1_ring, z2_ring, y_ring = (
                sb5(n) for n in ("out_ring", "h2_ring", "h2t_ring", "z1_ring", "z2_ring", "y_ring"))
            ps_turn, ps_1, ps_2, ps_3 = ([scope.enter_context(nc.psum_tensor(f"ps_{n}{k}", [P, NC], F32))
                                          for k in range(2)] for n in ("t", "one", "two", "three"))
            conv_step, conv_ready, conv_turned, x1_ready = (
                sem5(n) for n in ("conv_step", "conv_ready", "conv_turned", "x1_ready"))
            var2_ok, root2_ok, norm2_ok, dve_step = (sem5(n) for n in ("var2_ok", "root2_ok", "norm2_ok", "dve2_step"))
            h2_ready, h2_turned, h2t_ready = (sem5(n) for n in ("h2_ready", "h2_turned", "h2t_ready"))
            m1_ready, z1_ready, m2_ready, z2_ready = (sem5(n) for n in ("m1_ready", "z1_ready", "m2_ready", "z2_ready"))
            m3_ready, y_ready = (sem5(n) for n in ("m3_ready", "y_ready"))
            y_out = [sem5(f"y_out{k}") for k in range(2)]

            def chunk_of_x(c):
                return xs[:, c * BC:(c + 1) * BC, :].rearrange("p b f -> p (b f)")

            with nc.Block() as block:
                @block.vector
                def _(v):
                    chain = [0]

                    def link(ins):
                        chain[0] += 1
                        ins.then_inc(dve_step, 1)
                        v.wait_ge(dve_step, chain[0])

                    def add_conv(c):
                        v.wait_ge(conv_turned, c + 1)
                        v.scalar_tensor_tensor(out=chunk_of_x(c), in0=ps_turn[c % 2][:], scalar=0.0,
                                               in1=chunk_of_x(c), op0=ALU.max, op1=ALU.add).then_inc(x1_ready, 1)
                        v.wait_ge(x1_ready, c + 1)
                        for b in range(c * BC, (c + 1) * BC):
                            ins = v.bn_stats(stats[:, b, :], xs[:, b, :])
                        return ins

                    for c in range(CHUNKS):
                        n = slice(c * NC, (c + 1) * NC)
                        o = out_ring[:, c % 2, :]
                        if c >= 2:
                            v.wait_ge(conv_turned, c - 1)
                        v.tensor_tensor(o, h_t[:, n], dinv[:, n], ALU.mult).then_inc(conv_step, 1)
                        v.wait_ge(conv_step, 2 * c + 1)
                        v.tensor_tensor(o, o, acc[:, 0, n], ALU.add).then_inc(conv_step, 1)
                        v.wait_ge(conv_step, 2 * c + 2)
                        v.tensor_tensor(o, o, dinv[:, n], ALU.mult).then_inc(conv_ready, 1)
                        if c >= 1:
                            add_conv(c - 1)
                    link(add_conv(CHUNKS - 1))
                    layer_norm_stats(v, link, var2_ok, root2_ok, norm2_ok)

                    for s in range(CHUNKS + 3):
                        if s < CHUNKS:
                            v.wait_ge(h2_turned, s + 1)
                            if s >= 2:
                                v.wait_ge(m1_ready, s - 1)
                            v.tensor_copy(h2t_ring[:, s % 2, :], ps_turn[s % 2][:]).then_inc(h2t_ready, 1)
                        if s >= 3:
                            c = s - 3
                            v.wait_ge(m3_ready, c + 1)
                            if c >= 2:
                                v.wait_ge(y_out[c % 2], 16 * (c // 2))
                            v.tensor_tensor(y_ring[:, c % 2, :], ps_3[c % 2][:], chunk_of_x(c), ALU.add)\
                             .then_inc(y_ready, 1)

                @block.scalar
                def _(act):
                    act.wait_ge(var2_ok, 1)
                    act.activation(rstd[:], var[:], ACT.Sqrt, bias=eps_col[:]).then_inc(root2_ok, 1)
                    act.wait_ge(norm2_ok, 1)
                    for s in range(CHUNKS + 2):
                        if s < CHUNKS:
                            if s >= 2:
                                act.wait_ge(h2_turned, s - 1)
                            for k in range(BC):
                                n = s * BC + k
                                ins = act.activation(h2_ring[:, s % 2, k * P:(k + 1) * P], xs[:, n, :], ACT.Relu,
                                                     scale=rstd[:, n:n + 1], bias=shift[:, n:n + 1])
                            ins.then_inc(h2_ready, 1)
                        if 1 <= s <= CHUNKS:
                            c = s - 1
                            act.wait_ge(m1_ready, c + 1)
                            if c >= 2:
                                act.wait_ge(m2_ready, c - 1)
                            act.activation(z1_ring[:, c % 2, :], ps_1[c % 2][:], ACT.Relu, bias=b1u[:])\
                               .then_inc(z1_ready, 1)
                        if s >= 2:
                            c = s - 2
                            act.wait_ge(m2_ready, c + 1)
                            if c >= 2:
                                act.wait_ge(m3_ready, c - 1)
                            act.activation(z2_ring[:, c % 2, :], ps_2[c % 2][:], ACT.Relu, bias=B2)\
                               .then_inc(z2_ready, 1)

                @block.tensor
                def _(pe):
                    def turn(target, ring, c):
                        for k in range(BC):
                            ins = pe.transpose(target[:, k * P:(k + 1) * P], ring[:, c % 2, k * P:(k + 1) * P],
                                               ident[:])
                        return ins

                    for c in range(CHUNKS):
                        pe.wait_ge(conv_ready, c + 1)
                        if c >= 2:
                            pe.wait_ge(x1_ready, c - 1)
                        turn(ps_turn[c % 2], out_ring, c).then_inc(conv_turned, 1)
                    pe.wait_ge(x1_ready, CHUNKS)
                    for s in range(CHUNKS + 3):
                        if s < CHUNKS:
                            pe.wait_ge(h2_ready, s + 1)
                            if s >= 2:
                                pe.wait_ge(h2t_ready, s - 1)
                            turn(ps_turn[s % 2], h2_ring, s).then_inc(h2_turned, 1)
                        if 1 <= s <= CHUNKS:
                            c = s - 1
                            pe.wait_ge(h2t_ready, c + 1)
                            if c >= 2:
                                pe.wait_ge(z1_ready, c - 1)
                            pe.matmul(ps_1[c % 2][:], w1_sb[:, 0, :], h2t_ring[:, c % 2, :], start=True, stop=False)
                            pe.matmul(ps_1[c % 2][:], w1_sb[:, 1, :], acc[:, 1, c * NC:(c + 1) * NC],
                                      start=False, stop=True).then_inc(m1_ready, 1)
                        if 2 <= s <= CHUNKS + 1:
                            c = s - 2
                            pe.wait_ge(z1_ready, c + 1)
                            if c >= 2:
                                pe.wait_ge(z2_ready, c - 1)
                            pe.matmul(ps_2[c % 2][:], w2_sb[:], z1_ring[:, c % 2, :], start=True,
                                      stop=True).then_inc(m2_ready, 1)
                        if s >= 3:
                            c = s - 3
                            pe.wait_ge(z2_ready, c + 1)
                            if c >= 2:
                                pe.wait_ge(y_ready, c - 1)
                            for k in range(BC):
                                part = slice(k * P, (k + 1) * P)
                                pe.matmul(ps_3[c % 2][:, part], z2_ring[:, c % 2, part], w3_sb[:], start=True,
                                          stop=False)
                                ins = pe.matmul(ps_3[c % 2][:, part], ones_row[:], b3_row[:], start=False, stop=True)
                            ins.then_inc(m3_ready, 1)

                @block.sync
                def _(sp):
                    for c in range(CHUNKS):
                        sp.wait_ge(y_ready, c + 1)
                        rows_of = y_ring[:, c % 2, :].rearrange("p (b f) -> p b f", b=BC)
                        if c < CHUNKS - 1:
                            sp.dma_start(out_full[:, c * BC:(c + 1) * BC, :], rows_of).then_inc(y_out[c % 2], 16)
                        else:
                            sp.dma_start(out[FB * P:N, :], rows_of[0:TAILN, 0, :]).then_inc(y_out[c % 2], 16)
                    for k in range(2):
                        sp.wait_ge(y_out[k], 16 * ((CHUNKS - k + 1) // 2))


_INS = ['x', 'src', 'dst', 'edge_attr_128', 'L0_gnn_W', 'L0_gnn_b', 'L0_gnn_gamma', 'L0_gnn_beta', 'L1_gnn_u',
        'L1_gnn_W1', 'L1_gnn_b1', 'L1_gnn_W2', 'L1_gnn_b2', 'L1_gnn_W3', 'L1_gnn_b3']
_OUTS = [((6250, 128), 'float32')]


def kernel(**inputs):
    import numpy as _np
    import concourse.bacc as _bacc
    from concourse import mybir as _mybir
    from concourse.bass_utils import run_bass_kernel_spmd as _run

    nc = _bacc.Bacc("TRN2", target_bir_lowering=False, num_devices=1)
    arrays, args = {}, []
    for name in _INS:
        a = _np.ascontiguousarray(inputs[name])
        arrays[f"in_{name}_dram"] = a
        args.append(nc.dram_tensor(f"in_{name}_dram", a.shape, _mybir.dt.from_np(a.dtype), kind="ExternalInput").ap())
    for i, (shape, dtype) in enumerate(_OUTS):
        dt = _mybir.dt.from_np(_np.dtype(dtype))
        args.append(nc.dram_tensor(f"out_{i}_dram", shape, dt, kind="ExternalOutput").ap())
    gnn_kernel(nc, *args)
    r = _run(nc, [arrays], core_ids=[0])
    got = tuple(r.results[0][f"out_{i}_dram"] for i in range(len(_OUTS)))
    return got[0]
```

```python
from contextlib import ExitStack

import concourse.bass as bass
from concourse import mybir

F32 = mybir.dt.float32
F32R = mybir.dt.float32r
BF16 = mybir.dt.bfloat16
F16 = mybir.dt.float16
I32 = mybir.dt.int32
ALU = mybir.AluOpType
ACT = mybir.ActivationFunctionType
AX = mybir.AxisListType

P = 128
TILE = 128
GT = 4
W = 32
WT = 8
CG = 4
CT = CG * GT
WC = 96
DPI = 2
NG1 = CG
NG2 = DPI * CG
NGS = NG1 + NG2
HOTS = 4
EPS = 1e-5
TABLE = F16
NOWHERE = 1.0e6
FAR = NOWHERE / 4


def gnn_kernel(nc, x, src, dst, edge_attr, w_gcn, b_gcn, gamma, beta, u, w1, b1, w2, b2, w3, b3, out):
    N, D = x.shape
    E = src.shape[0]
    assert D == P and WT * CT == P
    NC = 512
    BC = NC // P
    NB = -(-N // P)
    CHUNKS = -(-NB // BC)
    FB = N // P
    TAILN = N - FB * P
    GE = GT * TILE
    FULL = E // GE
    OVER = (FULL + 1) * GE - E
    STEPS = -(-(FULL + 1) // NGS)
    NG = STEPS * NGS
    GG = STEPS * NG1
    DG = NG - GG
    DCH = DG // CG
    DT = DG * GT
    RC = -(-NG // P)
    RD = GG // P
    AW = N + WC
    BNC = 250
    KEYS = NB * WT
    assert N % BNC == 0 and E % GE and FB == NB - 1 == (CHUNKS - 1) * BC and AW >= NB * P
    assert 3 * RC * GE <= NB * P and RC * P <= 512 and KEYS <= 512 and STEPS % 2 == 0

    def width(c):
        return min(BC, NB - c * BC)

    table = nc.dram_tensor("scaled_h_table", (NB * P, P), F32, kind="Internal").ap()
    src_rows = src[0:FULL * GE].rearrange("(g e) -> g e", e=GE)
    dst_rows = dst[0:FULL * GE].rearrange("(g e) -> g e", e=GE)
    src_last = src[E - GE:E].rearrange("(a e) -> a e", a=1)
    dst_last = dst[E - GE:E].rearrange("(a e) -> a e", a=1)
    attr_groups = edge_attr[0:FULL * GE, :].rearrange("(g p t) f -> g p (t f)", p=P, t=GT)
    attr_last = edge_attr[E - GE:E, :].rearrange("(p t) f -> p (t f)", t=GT)
    x_full = x[0:FB * P, :].rearrange("(b p) f -> p b f", p=P)
    table_blocks = table.rearrange("(b p) f -> p b f", p=P)
    out_full = out[0:FB * P, :].rearrange("(b p) f -> p b f", p=P)

    with ExitStack() as ctx:
        def sb(name, shape, dt=F32, scope=ctx):
            return scope.enter_context(nc.sbuf_tensor(name, shape, dt))

        def bank(name, shape, scope):
            return scope.enter_context(nc.psum_tensor(name, shape, F32))

        def sem(name, scope):
            return scope.enter_context(nc.semaphore(name))

        def chained(v, steps):
            count = [0]

            def link(ins):
                count[0] += 1
                ins.then_inc(steps, 1)
                v.wait_ge(steps, count[0])
            return link

        dinv = sb("dinv", [P, NB])
        table_sb = sb("table_sb", [P, NB, 2, P], F32R)
        acc = sb("acc", [P, 2, AW])
        mean = sb("mean", [P, NB])
        var = sb("var", [P, NB])
        rstd = sb("rstd", [P, NB])
        shift = sb("shift", [P, NB])
        rel = sb("rel", [P, NG, GT])
        src_t = sb("src_t", [P, GG, GT])
        drel = sb("drel", [P, DG, GT])
        src_lo = sb("src_lo", [P, DG, GT], TABLE)
        src_hi = sb("src_hi", [P, DG, GT], F16)
        key = sb("key", [P, DG, GT], TABLE)
        inside = sb("inside", [P, DG, GT], F16)
        prel0 = sb("prel0", [P, DCH])
        prel = sb("prel", [P, DCH])
        starts = sb("starts", [1, STEPS + 1, 16])
        starts_int = sb("starts_int", [1, STEPS + 1, 16], I32)
        chunk_start0 = sb("chunk_start0", [1, DCH])
        span_int = sb("span_int", [1, 2], I32)
        iota_c = sb("iota_c", [P, WC])
        iota_lo = sb("iota_lo", [P, P], F16)
        iota_key = sb("iota_key", [P, KEYS], F16)
        ident = sb("ident", [P, P])
        ones_row = sb("ones_row", [1, P])
        ones_col = sb("ones_col", [P, 1], BF16)
        eps_col = sb("eps_col", [P, 1])
        w1_sb = sb("w1_sb", [P, 3, P])
        w2_sb = sb("w2_sb", [P, P])
        w3_sb = sb("w3_sb", [P, P])
        b3_row = sb("b3_row", [1, P])
        cols = sb("cols", [P, 6])
        B_GCN, GAMMA, BETA, B1, B2, U = (cols[:, k:k + 1] for k in range(6))
        b1u = sb("b1u", [P, 1])
        bn = sb("bn", [P, 8])

        def layer_norm_stats(v, link, stats, var_ready, root_ready, norm_ready):
            m0, m1, s0, s1 = stats[:, :, 1], stats[:, :, 4], stats[:, :, 2], stats[:, :, 5]
            v.tensor_tensor(mean[:], m0, m1, ALU.add)
            v.tensor_tensor(shift[:], m0, m1, ALU.subtract)
            link(v.tensor_tensor(rstd[:], s0, s1, ALU.add))
            v.tensor_scalar(mean[:], mean[:], 0.5, None, ALU.mult)
            link(v.scalar_tensor_tensor(out=shift[:], in0=shift[:], scalar=0.25, in1=shift[:],
                                        op0=ALU.mult, op1=ALU.mult))
            v.scalar_tensor_tensor(out=var[:], in0=rstd[:], scalar=1.0 / P, in1=shift[:],
                                   op0=ALU.mult, op1=ALU.add).then_inc(var_ready, 1)
            v.wait_ge(root_ready, 1)
            link(v.reciprocal(rstd[:], rstd[:]))
            v.scalar_tensor_tensor(out=shift[:], in0=mean[:], scalar=-1.0, in1=rstd[:],
                                   op0=ALU.mult, op1=ALU.mult).then_inc(norm_ready, 1)

        early = ExitStack()
        h_t = sb("h_t", [P, NB * P], scope=early)
        degree = acc[0:1, :, :]

        with ExitStack() as scope:
            space = acc[:].rearrange("p a n -> p (a n)")
            xs = space[:, 0:NB * P].rearrange("p (b f) -> p b f", f=P)
            raw, edge_f, unmasked = (space[:, NB * P + k * RC * GE:NB * P + (k + 1) * RC * GE]
                                     .rearrange("p (c e) -> p c e", c=RC) for k in range(3))
            raw = raw.bitcast(I32)
            raw_last = sb("raw_last", [1, GE], I32, scope)
            last_f = sb("last_f", [1, GE], scope=scope)
            tile_min = sb("tile_min", [P, RC, GT], scope=scope)
            tile_max = sb("tile_max", [P, RC, GT], scope=scope)
            group_lim = sb("group_lim", [P, 2, RC], scope=scope)
            spans = sb("spans", [P, 2, RC * GT], scope=scope)
            span_cols = sb("span_cols", [P, 2], scope=scope)
            span_row = sb("span_row", [1, 8], scope=scope)
            group_rows = sb("group_rows", [1, 2, NG], scope=scope)
            chunk_max = sb("chunk_max", [1, NG // CG], scope=scope)
            chunk_min = sb("chunk_min", [1, NG // CG], scope=scope)
            tile_row = sb("tile_row", [1, DG, GT], scope=scope)
            band = sb("band", [1, 2 * P], scope=scope)
            nodes_row = sb("nodes_row", [1, P], scope=scope)
            minus_start = sb("minus_start", [1, DCH], scope=scope)
            lo_int = sb("lo_int", [P, DG, GT], I32, scope)
            hi_int = sb("hi_int", [P, DG, GT], I32, scope)
            stats = sb("stats", [P, NB, 6], scope=scope)
            w_raw = sb("w_raw", [P, P], scope=scope)
            wg_t = sb("wg_t", [P, P], scope=scope)
            h_ring = sb("h_ring", [P, 2, BC, P], scope=scope)
            ht_ring = sb("ht_ring", [P, 2, NC], scope=scope)
            bstats = sb("bstats", [P, N // BNC, 6], scope=scope)
            turn = [bank(f"turn{k}", [P, GT, P], scope) for k in range(2)]
            ps_turn = [bank(f"ps_turn{k}", [P, BC, P], scope) for k in range(2)]
            ps_lin = [bank(f"ps_lin{k}", [P, NC], scope) for k in range(2)]
            ps_row = bank("ps_row", [P, 512], scope)
            ps_small = bank("ps_small", [P, 512], scope)

            (x_in, dst_in, src_in, last_in, w_in, dst_cast, src_cast, last_put, zeroed, ident_ok, consts, turned,
             dst_read, src_read, limits, rows_t, spread, spread_read, dve_step, var_ok, root_ok, norm_ok,
             h_ready, h_turned, ht_ready, lin_ready, lin_saved, w_turned, wg_ready, b1u_done, bvar_ok, broot_ok
             ) = (sem(n, scope) for n in
                  "x_in dst_in src_in last_in w_in dst_cast src_cast last_put zeroed ident_ok consts turned "
                  "dst_read src_read limits rows_t spread spread_read ln_step var_ok root_ok norm_ok "
                  "h_ready h_turned ht_ready lin_ready lin_saved w_turned wg_ready b1u_done bvar_ok broot_ok".split())
            W_LOADS = 11
            CONSTS = 7

            def rows(c):
                return min(P, FULL + 1 - c * P)

            turns = [("dst", c, True) for c in range(RC)] + [("dst", c, False) for c in range(RD, RC)]
            DST_TURNS = len(turns)
            turns += [("src", c, True) for c in range(RD + 1)] + [("src", c, False) for c in range(RD, RC)]

            def dense_part(c):
                first = max(0, GG - c * P)
                return first, c * P + first - GG

            with nc.Block() as block:
                @block.sync
                def _(sp):
                    last = FULL - (RC - 1) * P

                    def load_rows(view, arrived):
                        for c in range(RC):
                            n = min(P, FULL - c * P)
                            sp.dma_start(raw[0:n, c, :], view[c * P:c * P + n, :]).then_inc(arrived, 16)

                    load_rows(dst_rows, dst_in)
                    sp.dma_start(raw_last[:], dst_last).then_inc(last_in, 16)
                    sp.dma_start(xs[:, 0:FB, :], x_full).then_inc(x_in, 16)
                    sp.wait_ge(zeroed, 1)
                    sp.dma_start(xs[0:TAILN, FB, :], x[FB * P:N, :]).then_inc(x_in, 16)
                    sp.dma_start(w_raw[:], w_gcn).then_inc(w_in, 16)
                    for k, vec in enumerate((b_gcn, gamma, beta, b1, b2)):
                        sp.dma_start(cols[:, k:k + 1], vec.rearrange("(p a) -> p a", a=1)).then_inc(w_in, 16)
                    sp.dma_start(U, u[0:1, :].rearrange("a p -> p a")).then_inc(w_in, 16)
                    sp.dma_start(w1_sb[:], w1.rearrange("(k p) n -> p k n", p=P)).then_inc(w_in, 16)
                    sp.dma_start(w2_sb[:], w2).then_inc(w_in, 16)
                    sp.dma_start(w3_sb[:], w3).then_inc(w_in, 16)
                    sp.dma_start(b3_row[:], b3.rearrange("(a n) -> a n", a=1)).then_inc(w_in, 16)
                    sp.wait_ge(dst_cast, 2)
                    sp.dma_start(edge_f[last:last + 1, RC - 1, :], last_f[:]).then_inc(last_put, 16)
                    load_rows(src_rows, src_in)
                    sp.dma_start(raw[last:last + 1, RC - 1, :], src_last).then_inc(src_in, 16)
                    sp.wait_ge(last_put, 16)
                    sp.wait_ge(src_in, 16 * (RC + 1))

                @block.gpsimd
                def _(pool):
                    pool.memset(xs[:, FB:NB, :], 0.0).then_inc(zeroed, 1)
                    pool.memset(ident[:], 0.0).then_inc(consts, 1)
                    pool.wait_ge(consts, 1)
                    pool.affine_select(out=ident[:], in_=ident[:], compare_op=ALU.not_equal, fill=1.0, base=0,
                                       pattern=[[-1, P]], channel_multiplier=1).then_inc(ident_ok, 1)
                    for target, pattern in ((iota_c, [[1, WC]]), (iota_lo, [[1, P]]), (iota_key, [[1, KEYS]]),
                                            (nodes_row, [[0, CT], [1, WT]])):
                        pool.iota(target[:], pattern, base=0, channel_multiplier=0,
                                  allow_small_or_imprecise_dtypes=True).then_inc(consts, 1)
                    pool.memset(ones_row[:], 1.0).then_inc(consts, 1)
                    pool.memset(ones_col[:], 1.0).then_inc(consts, 1)
                    pool.wait_ge(consts, CONSTS)

                @block.vector
                def _(v):
                    link = chained(v, dve_step)
                    v.memset(tile_min[:], FAR)
                    v.memset(tile_max[:], 0.0)
                    v.memset(group_rows[:, 0, :], FAR)
                    v.memset(group_rows[:, 1, :], 0.0)
                    v.memset(tile_row[:], FAR)
                    v.memset(span_cols[:], 0.0)
                    v.memset(starts[:], 0.0)
                    v.memset(rel[:], NOWHERE)
                    v.memset(drel[:], NOWHERE)
                    v.memset(lo_int[:], 0)
                    v.memset(band[:], 0.0)
                    link(v.memset(eps_col[:], EPS))
                    v.memset(band[:, P:P + WT], 1.0)
                    v.wait_ge(last_in, 16)
                    link(v.tensor_copy(last_f[:], raw_last[:]))
                    v.memset(last_f[:, 0:OVER], NOWHERE).then_inc(dst_cast, 1)
                    v.wait_ge(dst_in, 16 * RC)
                    for c in range(RC):
                        n = min(P, FULL - c * P)
                        ins = v.tensor_copy(edge_f[0:n, c, :], raw[0:n, c, :])
                    ins.then_inc(dst_cast, 1)
                    v.wait_ge(dst_cast, 2)
                    v.wait_ge(last_put, 16)
                    for c in range(RC):
                        r = rows(c)
                        v.tensor_reduce(tile_min[0:r, c, :], edge_f[0:r, c, :].rearrange("g (t e) -> g t e", t=GT),
                                        AX.X, ALU.min)
                        ins = v.scalar_tensor_tensor(out=unmasked[0:r, c, :], in0=edge_f[0:r, c, :],
                                                     scalar=NOWHERE / 2, in1=edge_f[0:r, c, :],
                                                     op0=ALU.is_lt, op1=ALU.mult)
                    link(ins)
                    for c in range(RC):
                        r = rows(c)
                        ins = v.tensor_reduce(tile_max[0:r, c, :],
                                              unmasked[0:r, c, :].rearrange("g (t e) -> g t e", t=GT), AX.X, ALU.max)
                    link(ins)
                    v.tensor_reduce(group_lim[:, 0, :], tile_min[:], AX.X, ALU.min)
                    v.tensor_reduce(group_lim[:, 1, :], tile_max[:], AX.X, ALU.max)
                    link(v.tensor_tensor(spans[:, 0, :], tile_max[:].rearrange("p c t -> p (c t)"),
                                         tile_min[:].rearrange("p c t -> p (c t)"), ALU.subtract))
                    link(v.tensor_tensor(spans[:, 1, 0:RC], group_lim[:, 1, :], group_lim[:, 0, :], ALU.subtract))
                    v.tensor_reduce(span_cols[:, 0:1], spans[:, 0, :], AX.X, ALU.max)
                    v.tensor_reduce(span_cols[:, 1:2], spans[:, 1, 0:RC], AX.X, ALU.max).then_inc(limits, 1)

                    def save_dst(t):
                        _, c, grouped = turns[t]
                        v.wait_ge(turned, t + 1)
                        if grouped:
                            target, first = rel[:, c * P:c * P + rows(c), :], 0
                        else:
                            first, place = dense_part(c)
                            target = drel[:, place:place + rows(c) - first, :]
                        v.tensor_copy(target.rearrange("p g t -> p t g"), turn[t % 2][:, :, first:rows(c)])\
                         .then_inc(dst_read, 1)

                    for t in range(DST_TURNS):
                        save_dst(t)
                    v.wait_ge(rows_t, 1)
                    for c in range(RC):
                        v.tensor_copy(group_rows[:, 0, c * P:c * P + rows(c)], ps_row[0:1, c * P:c * P + rows(c)])
                    v.wait_ge(rows_t, 2)
                    for c in range(RC):
                        v.tensor_copy(group_rows[:, 1, c * P:c * P + rows(c)], ps_small[0:1, c * P:c * P + rows(c)])
                    v.wait_ge(rows_t, 3)
                    v.tensor_reduce(span_row[:, 0:1], ps_lin[0][0:1, 0:P], AX.X, ALU.max)
                    link(v.tensor_reduce(span_row[:, 1:2], ps_lin[0][0:1, P:2 * P], AX.X, ALU.max))
                    ps_tiles = {RD: ps_lin[1], RD + 1: ps_turn[0], RD + 2: ps_turn[1]}
                    for c in range(RD, RC):
                        v.wait_ge(rows_t, 4 + c - RD)
                        first, place = dense_part(c)
                        ps = ps_tiles[c]
                        ps = ps[:].rearrange("p b n -> p (b n)") if c > RD else ps[:]
                        ins = v.tensor_copy(
                            tile_row[:, place:place + rows(c) - first, :].rearrange("a g t -> a t g"),
                            ps[0:1, :].rearrange("a (t g) -> a t g", t=GT)[:, :, first:rows(c)])
                    link(ins)
                    v.tensor_reduce(chunk_min[:], group_rows[:, 0, :].rearrange("a (c g) -> a c g", g=CG), AX.X, ALU.min)
                    link(v.tensor_reduce(chunk_max[:], group_rows[:, 1, :].rearrange("a (c g) -> a c g", g=CG),
                                         AX.X, ALU.max))
                    d0 = GG // CG
                    link(v.tensor_tensor(chunk_max[:], chunk_max[:], chunk_min[:], ALU.subtract))
                    v.tensor_scalar(minus_start[:], chunk_min[:, d0:], -1.0, None, ALU.mult)
                    v.tensor_copy(chunk_start0[:], chunk_min[:, d0:])
                    link(v.tensor_reduce(span_row[:, 2:3], chunk_max[:, d0:], AX.X, ALU.max))
                    link(v.tensor_scalar(span_row[:, 3:4], span_row[:, 0:1], float(W // WT), None, ALU.mult))
                    link(v.tensor_tensor(span_row[:, 1:2], span_row[:, 1:2], span_row[:, 3:4], ALU.max))
                    link(v.tensor_scalar(span_row[:, 1:3], span_row[:, 1:3], 0.0, None, ALU.max))
                    v.tensor_copy(span_int[:], span_row[:, 1:3])
                    v.tensor_scalar(starts[:, 0:STEPS, 0:NG1],
                                    group_rows[:, 0, 0:GG].rearrange("a (s g) -> a s g", g=NG1), -float(W), None,
                                    ALU.add)
                    v.tensor_scalar(starts[:, 0:STEPS, NG1:NGS],
                                    group_rows[:, 0, GG:].rearrange("a (s g) -> a s g", g=NG2), -float(W), None,
                                    ALU.add).then_inc(limits, 1)
                    v.wait_ge(spread, 1)
                    link(v.tensor_tensor(rel[:], rel[:], ps_row[:, 0:NG].unsqueeze(2).to_broadcast([P, NG, GT]),
                                         ALU.subtract))
                    v.tensor_scalar(rel[:], rel[:], float(W), None, ALU.add)
                    flat = drel[:].rearrange("p g t -> p (g t)")
                    SPREADS = -(-DT // 512)
                    for k in range(SPREADS):
                        n = slice(k * 512, min(DT, (k + 1) * 512))
                        v.wait_ge(spread, 2 + k)
                        ins = v.tensor_tensor(flat[:, n], flat[:, n], turn[k % 2][:].rearrange("p t n -> p (t n)")
                                              [:, 0:n.stop - n.start], ALU.subtract)
                        ins.then_inc(spread_read, 1)
                    v.wait_ge(spread_read, SPREADS)
                    v.tensor_scalar(drel[:], drel[:], float(WT), None, ALU.add)
                    v.wait_ge(spread, 2 + SPREADS)
                    v.tensor_scalar(prel0[:], ps_small[:, 0:DCH], -float(WT), None, ALU.add).then_inc(spread_read, 1)
                    v.wait_ge(w_turned, 1)
                    v.tensor_copy(wg_t[:], ps_small[:, 128:256]).then_inc(wg_ready, 1)

                    v.wait_ge(x_in, 32)
                    for b in range(NB):
                        ins = v.bn_stats(stats[:, b, :], xs[:, b, :])
                    link(ins)
                    layer_norm_stats(v, link, stats, var_ok, root_ok, norm_ok)

                    for c in range(CHUNKS):
                        n = width(c)
                        v.wait_ge(h_turned, c + 1)
                        if c >= 2:
                            v.wait_ge(lin_ready, c - 1)
                        v.tensor_copy(ht_ring[:, c % 2, 0:n * P], ps_turn[c % 2][:, 0:n, :].rearrange(
                            "p b n -> p (b n)")).then_inc(ht_ready, 1)

                    v.wait_ge(src_read, len(turns) - DST_TURNS)
                    link(v.tensor_single_scalar(hi_int[:], lo_int[:], 7, ALU.logical_shift_right))
                    link(v.tensor_single_scalar(lo_int[:], lo_int[:], P - 1, ALU.bitwise_and))
                    v.tensor_copy(src_lo[:], lo_int[:])
                    v.tensor_scalar(src_hi[:], hi_int[:], float(WT), None, ALU.mult)

                    v.wait_ge(lin_saved, CHUNKS)
                    for c in range(N // BNC):
                        ins = v.bn_stats(bstats[:, c, :], h_t[:, c * BNC:(c + 1) * BNC])
                    link(ins)
                    v.bn_aggr(bn[:, 0:2], bstats[:].rearrange("p c s -> p (c s)")).then_inc(bvar_ok, 1)
                    v.wait_ge(broot_ok, 1)
                    link(v.reciprocal(bn[:, 3:4], bn[:, 2:3]))
                    link(v.tensor_tensor(bn[:, 4:5], bn[:, 3:4], GAMMA, ALU.mult))
                    link(v.tensor_tensor(bn[:, 5:6], bn[:, 0:1], bn[:, 4:5], ALU.mult))
                    link(v.tensor_tensor(bn[:, 6:7], BETA, bn[:, 5:6], ALU.subtract))
                    v.tensor_scalar(h_t[:], h_t[:], bn[:, 4:5], bn[:, 6:7], ALU.mult, ALU.add)
                    v.wait_ge(b1u_done, 1)
                    v.tensor_tensor(b1u[:], ps_small[:, 448:449], B1, ALU.add)

                @block.scalar
                def _(act):
                    act.wait_ge(src_in, 16 * (RC + 1))
                    act.wait_ge(turned, DST_TURNS)
                    act.wait_ge(limits, 1)
                    for c in range(RC):
                        ins = act.copy(edge_f[0:rows(c), c, :], raw[0:rows(c), c, :])
                    ins.then_inc(src_cast, 1)
                    for t in range(DST_TURNS, len(turns)):
                        _, c, grouped = turns[t]
                        act.wait_ge(turned, t + 1)
                        if grouped:
                            n = min(P, GG - c * P)
                            first, target = 0, src_t[:, c * P:c * P + n, :]
                        else:
                            first, place = dense_part(c)
                            n = rows(c)
                            target = lo_int[:, place:place + n - first, :]
                        act.copy(target.rearrange("p g t -> p t g"), turn[t % 2][:, :, first:n]).then_inc(src_read, 1)
                    act.wait_ge(var_ok, 1)
                    act.activation(rstd[:], var[:], ACT.Sqrt, bias=eps_col[:]).then_inc(root_ok, 1)
                    act.wait_ge(norm_ok, 1)
                    act.wait_ge(w_in, 16 * W_LOADS)
                    for c in range(CHUNKS + 1):
                        if c < CHUNKS:
                            if c >= 2:
                                act.wait_ge(h_turned, c - 1)
                            for k in range(width(c)):
                                n = c * BC + k
                                ins = act.activation(h_ring[:, c % 2, k, :], xs[:, n, :], ACT.Relu,
                                                     scale=rstd[:, n:n + 1], bias=shift[:, n:n + 1])
                            ins.then_inc(h_ready, 1)
                        if c >= 1:
                            n = width(c - 1) * P
                            act.wait_ge(lin_ready, c)
                            act.activation(h_t[:, (c - 1) * NC:(c - 1) * NC + n], ps_lin[(c - 1) % 2][:, 0:n],
                                           ACT.Identity, bias=B_GCN).then_inc(lin_saved, 1)
                    act.wait_ge(bvar_ok, 1)
                    act.activation(bn[:, 2:3], bn[:, 1:2], ACT.Sqrt, bias=eps_col[:]).then_inc(broot_ok, 1)

                @block.tensor
                def _(pe):
                    def turn_rows(t):
                        _, c, grouped = turns[t]
                        if t >= 2:
                            pe.wait_ge(*((dst_read, t - 1) if t - 2 < DST_TURNS else (src_read, t - 1 - DST_TURNS)))
                        r = rows(c)
                        order = "g (p t) -> g t p" if grouped else "g (t p) -> g t p"
                        for j in range(GT):
                            ins = pe.transpose(turn[t % 2][:, j, 0:r],
                                               edge_f[0:r, c, :].rearrange(order, t=GT)[:, j, :], ident[0:r, 0:r])
                        ins.then_inc(turned, 1)

                    pe.wait_ge(ident_ok, 1)
                    pe.wait_ge(dst_cast, 2)
                    pe.wait_ge(last_put, 16)
                    for t in range(DST_TURNS):
                        turn_rows(t)
                    pe.wait_ge(limits, 1)
                    for m, ps in ((0, ps_row), (1, ps_small)):
                        for c in range(RC):
                            ins = pe.transpose(ps[0:1, c * P:(c + 1) * P], group_lim[:, m, c:c + 1], ident[:])
                        ins.then_inc(rows_t, 1)
                    for m in range(2):
                        ins = pe.transpose(ps_lin[0][0:1, m * P:(m + 1) * P], span_cols[:, m:m + 1], ident[:])
                    ins.then_inc(rows_t, 1)
                    ps_tiles = {RD: ps_lin[1], RD + 1: ps_turn[0], RD + 2: ps_turn[1]}
                    for c in range(RD, RC):
                        ps = ps_tiles[c]
                        ps = ps[:].rearrange("p b n -> p (b n)") if c > RD else ps[:]
                        for t in range(GT):
                            ins = pe.transpose(ps[0:1, t * P:(t + 1) * P], tile_min[:, c, t:t + 1], ident[:])
                        ins.then_inc(rows_t, 1)
                    pe.wait_ge(consts, CONSTS)
                    pe.wait_ge(limits, 2)
                    pe.matmul(ps_row[:, 0:NG], ones_row[:], group_rows[:, 0, :], start=True, stop=True)\
                      .then_inc(spread, 1)
                    tiles = tile_row[:].rearrange("a g t -> a (g t)")
                    for k in range(-(-DT // 512)):
                        n = slice(k * 512, min(DT, (k + 1) * 512))
                        if k >= 2:
                            pe.wait_ge(spread_read, k - 1)
                        else:
                            pe.wait_ge(dst_read, DST_TURNS)
                        pe.matmul(turn[k % 2][:].rearrange("p t n -> p (t n)")[:, 0:n.stop - n.start], ones_row[:],
                                  tiles[:, n], start=True, stop=True).then_inc(spread, 1)
                    for t in range(CT):
                        pe.matmul(ps_small[:, 0:DCH], band[:, P - WT * t:2 * P - WT * t],
                                  tiles.rearrange("a (c t) -> a t c", t=CT)[:, t, :], start=(t == 0), stop=False)
                    pe.matmul(ps_small[:, 0:DCH], ones_row[:], minus_start[:], start=False, stop=False)
                    pe.matmul(ps_small[:, 0:DCH], nodes_row[:], ones_row[:, 0:DCH], start=False, stop=True)\
                      .then_inc(spread, 1)
                    pe.wait_ge(w_in, 16 * W_LOADS)
                    pe.wait_ge(spread_read, -(-DT // 512) + 1)
                    pe.transpose(ps_small[:, 128:256], w_raw[:], ident[:]).then_inc(w_turned, 1)
                    pe.wait_ge(src_cast, 1)
                    for t in range(DST_TURNS, len(turns)):
                        turn_rows(t)
                    pe.wait_ge(wg_ready, 1)
                    for c in range(CHUNKS + 1):
                        if c < CHUNKS:
                            pe.wait_ge(h_ready, c + 1)
                            if c >= 2:
                                pe.wait_ge(ht_ready, c - 1)
                            for k in range(width(c)):
                                ins = pe.transpose(ps_turn[c % 2][:, k, :], h_ring[:, c % 2, k, :], ident[:])
                            ins.then_inc(h_turned, 1)
                        if c >= 1:
                            n = width(c - 1) * P
                            pe.wait_ge(ht_ready, c)
                            if c >= 3:
                                pe.wait_ge(lin_saved, c - 2)
                            pe.matmul(ps_lin[(c - 1) % 2][:, 0:n], wg_t[:], ht_ring[:, (c - 1) % 2, 0:n], start=True,
                                      stop=True).then_inc(lin_ready, 1)
                    pe.matmul(ps_small[:, 448:449], w1_sb[:, 2, :], U, start=True, stop=True).then_inc(b1u_done, 1)

        span = nc.values_load(span_int[0:1, 0:1], min_val=0, max_val=N * (W // WT))
        chunk_span = nc.values_load(span_int[0:1, 1:2], min_val=0, max_val=N)
        passes = nc.snap(span // W + 1)
        chunk_passes = nc.snap(chunk_span // WC + 1)

        def group_hot(v, target, g, count, node_type_iota):
            offsets = rel[:, bass.ds(g, count), :].rearrange("p g t -> p (g t)")
            return v.tensor_tensor(target, offsets.unsqueeze(2).to_broadcast([P, count * GT, W]),
                                   node_type_iota.unsqueeze(1).to_broadcast([P, count * GT, W]), ALU.is_equal)

        with ExitStack() as scope:
            hot = [sb(f"deg_hot{k}", [P, NGS, GT, W], BF16, scope) for k in range(2)]
            counts = [bank(f"counts{k}", [P, 512], scope) for k in range(2)]
            hot_ready, counted, added, moved = (sem(f"deg_{n}", scope) for n in ("hot", "counted", "added", "moved"))
            with nc.Block() as block:
                @block.vector
                def _(v):
                    v.memset(degree, 0.0)
            with nc.Fori(0, passes):
                with nc.Block() as block:
                    @block.vector
                    def _(v):
                        for s in (hot_ready, counted, added, moved):
                            v.sem_clear(s)
                        v.tensor_scalar(rel[:], rel[:], -float(W), None, ALU.add)
                        v.tensor_scalar(starts[:, :, 0:NGS], starts[:, :, 0:NGS], float(W), None, ALU.add)\
                         .then_inc(moved, 1)
                        v.wait_ge(moved, 1)
                        v.tensor_scalar(starts_int[:], starts[:], float(N), None, ALU.min)
                with nc.Block() as block:
                    @block.vector
                    def _(v):
                        regs = [v.alloc_register(f"deg_start{k}") for k in range(NGS)]

                        def make_hot(s, b, reuse):
                            if reuse:
                                v.wait_ge(counted, s - 1)
                            group_hot(v, hot[b][:, 0:NG1].rearrange("p g t n -> p (g t) n"), s * NG1, NG1,
                                      iota_c[:, 0:W])
                            group_hot(v, hot[b][:, NG1:NGS].rearrange("p g t n -> p (g t) n"), GG + s * NG2, NG2,
                                      iota_c[:, 0:W]).then_inc(hot_ready, 1)

                        def add_counts(s, b, first):
                            v.load(regs, starts_int[0:1, bass.ds(s, 1), 0:NGS].rearrange("a s g -> a (s g)"))
                            v.wait_ge(counted, s + 1)
                            for k in range(NGS):
                                start = v.snap(regs[k], min_val=0, max_val=N)
                                if not (first and k < 2):
                                    v.wait_ge(added, s * NGS + k - 1)
                                win = degree[:, k % 2, bass.ds(start, W)]
                                v.tensor_tensor(win, win, counts[b][0:1, k * W:(k + 1) * W], ALU.add)\
                                 .then_inc(added, 1)

                        make_hot(0, 0, False)
                        make_hot(1, 1, False)
                        add_counts(0, 0, True)
                        with v.Fori(1, STEPS // 2) as i:
                            make_hot(2 * i, 0, True)
                            add_counts(2 * i - 1, 1, False)
                            make_hot(2 * i + 1, 1, True)
                            add_counts(2 * i, 0, False)
                        add_counts(STEPS - 1, 1, False)

                    @block.tensor
                    def _(pe):
                        def count(s, b, reuse):
                            pe.wait_ge(hot_ready, s + 1)
                            if reuse:
                                pe.wait_ge(added, (s - 1) * NGS)
                            for t in range(GT):
                                ins = pe.matmul(counts[b][0:1, 0:NGS * W], ones_col[:], hot[b][:, :, t, :],
                                                start=(t == 0), stop=(t == GT - 1))
                            ins.then_inc(counted, 1)
                        count(0, 0, False)
                        count(1, 1, False)
                        with pe.Fori(1, STEPS // 2) as i:
                            count(2 * i, 0, True)
                            count(2 * i + 1, 1, True)
            with nc.Fori(0, passes):
                with nc.Block() as block:
                    @block.vector
                    def _(v):
                        v.tensor_scalar(rel[:], rel[:], float(W), None, ALU.add)
                        v.tensor_scalar(starts[:, :, 0:NGS], starts[:, :, 0:NGS], -float(W), None, ALU.add)

        with ExitStack() as scope:
            row_ring = sb("row_ring", [P, 2, BC, P], scope=scope)
            ps_rows = [bank(f"ps_rows{k}", [P, BC, P], scope) for k in range(2)]
            ps_deg = bank("ps_deg", [P, 512], scope)
            deg_turned, deg_root, dinv_ok, h_back, row_ready, high_ready, low_ready = (
                sem(n, scope) for n in ("deg_turned", "deg_root", "dinv_ok", "h_back", "row_ready", "high_ready",
                                        "low_ready"))
            row_out = [sem(f"row_out{k}", scope) for k in range(2)]
            with nc.Block() as block:
                @block.tensor
                def _(pe):
                    for b in range(NB):
                        for k in range(2):
                            ins = pe.matmul(ps_deg[:, b:b + 1], degree[:, k, b * P:(b + 1) * P], ones_row[:, 0:1],
                                            start=(k == 0), stop=(k == 1))
                    ins.then_inc(deg_turned, 1)
                    for c in range(CHUNKS):
                        if c >= 2:
                            pe.wait_ge(row_ready, c - 1)
                        for k in range(width(c)):
                            b = c * BC + k
                            ins = pe.transpose(ps_rows[c % 2][:, k, :], h_t[:, b * P:(b + 1) * P], ident[:])
                        ins.then_inc(h_back, 1)

                @block.scalar
                def _(act):
                    act.wait_ge(deg_turned, 1)
                    act.activation(dinv[:], ps_deg[:, 0:NB], ACT.Sqrt, bias=1.0).then_inc(deg_root, 1)
                    for c in range(CHUNKS):
                        n = width(c)
                        act.wait_ge(row_ready, c + 1)
                        act.copy(table_sb[:, c * BC:c * BC + n, 0, :], row_ring[:, c % 2, 0:n, :])\
                           .then_inc(high_ready, 1)

                @block.vector
                def _(v):
                    v.wait_ge(deg_root, 1)
                    v.reciprocal(dinv[:], dinv[:]).then_inc(dinv_ok, 1)
                    v.wait_ge(dinv_ok, 1)

                    def low_part(c):
                        n = width(c)
                        v.wait_ge(high_ready, c + 1)
                        v.tensor_tensor(table_sb[:, c * BC:c * BC + n, 1, :], row_ring[:, c % 2, 0:n, :],
                                        table_sb[:, c * BC:c * BC + n, 0, :].bitcast(F32), ALU.subtract)\
                         .then_inc(low_ready, 1)

                    for c in range(CHUNKS):
                        n = width(c)
                        if c >= 2:
                            v.wait_ge(row_out[c % 2], 16 * (c // 2))
                            v.wait_ge(low_ready, c - 1)
                        v.wait_ge(h_back, c + 1)
                        v.tensor_tensor(row_ring[:, c % 2, 0:n, :], ps_rows[c % 2][:, 0:n, :],
                                        dinv[:, c * BC:c * BC + n].unsqueeze(2).to_broadcast([P, n, P]), ALU.mult)\
                         .then_inc(row_ready, 1)
                        if c >= 1:
                            low_part(c - 1)
                    low_part(CHUNKS - 1)

                @block.sync
                def _(sp):
                    for c in range(CHUNKS):
                        n = width(c)
                        sp.wait_ge(row_ready, c + 1)
                        sp.dma_start(table_blocks[:, c * BC:c * BC + n, :], row_ring[:, c % 2, 0:n, :])\
                          .then_inc(row_out[c % 2], 16)
                    for k in range(2):
                        sp.wait_ge(row_out[k], 16 * ((CHUNKS - k + 1) // 2))

        early.close()

        PHASE = ["g", "e", "e", "c", "g", "e", "e"]
        ITEMS = PHASE * DPI
        NI = len(ITEMS)
        AT = [CT * (j // len(PHASE)) + 2 * (j % len(PHASE)) for j in range(NI)]
        LAG = 3
        ATTR = [j for j in range(NI) if ITEMS[j] != "c"]
        GATH = [j for j in range(NI) if ITEMS[j] == "g"]
        DENSE = [j for j in range(NI) if ITEMS[j] == "e"]
        CHNK = [j for j in range(NI) if ITEMS[j] == "c"]
        PARTS = [b for b in range(2, CT)]
        BLOCKS_AT = {q: range(NB * k // len(PARTS), NB * (k + 1) // len(PARTS)) for k, q in enumerate(PARTS)}

        def start_of(j):
            return (GATH.index(j) if j in GATH else NG1 + DENSE.index(j) if j in DENSE else NGS + CHNK.index(j))

        def group_of(j, s):
            return s * NG1 + GATH.index(j) if j in GATH else GG + s * NG2 + DENSE.index(j)

        with ExitStack() as scope:
            counts_sb = [sb(f"counts_sb{k}", [P, NB, P], F32R, scope) for k in range(2)]
            lo_hot = sb("lo_hot", [P, HOTS, P], BF16, scope)
            key_hot = sb("key_hot", [P, HOTS, KEYS], BF16, scope)
            group_hots = sb("group_hots", [P, 2, GT, W], scope=scope)
            chunk_hot = sb("chunk_hot", [P, WC], scope=scope)
            product = sb("product", [P, 2, 2 * P], scope=scope)
            attr = sb("attr", [P, HOTS, GT * P], scope=scope)
            gathered = sb("gathered", [P, NG1, GT, P], scope=scope)
            index = sb("index", [P, NG1, GT], I32, scope)
            ps_counts = [bank(f"ps_counts{k}", [P, 2, 512], scope) for k in range(2)]
            ps_product = [bank(f"ps_product{k}", [P, 512], scope) for k in range(2)]
            ps_sums = [bank(f"ps_sums{k}", [P, 512], scope) for k in range(2)]
            tile_moved, moved, hot_ready, built, saved, multiplied, product_ready, index_ready, gathers_open = (
                sem(n, scope) for n in ("tile_moved", "moved", "hot_ready", "built", "saved", "multiplied",
                                        "product_ready", "index_ready", "gathers_open"))
            attr_in = [sem(f"attr_in{k}", scope) for k in range(HOTS)]
            gather_in = [sem(f"gather_in{k}", scope) for k in range(NG1)]
            item_hot = [sem(f"item_hot{j}", scope) for j in range(NI)]
            summed = [sem(f"summed{j}", scope) for j in range(NI)]
            added = [sem(f"added{j}", scope) for j in range(NI)]
            per_pass = (moved, hot_ready, built, saved, multiplied, product_ready, index_ready, gathers_open,
                        *attr_in, *gather_in, *item_hot, *summed, *added)

            def need(eng, semaphore, count):
                if not isinstance(count, int) or count > 0:
                    eng.wait_ge(semaphore, count)

            def nth(j, s):
                return s if ITEMS[j] == "c" else s + 1

            def before(j, k, s):
                if isinstance(s, int) and s == 0:
                    while j >= k and ITEMS[j - k] == "c":
                        k += k
                    return [(j - k, 1)] if j >= k else []
                i, t = (j - k, s) if j >= k else (j - k + NI, s - 1)
                return [(i, nth(i, t))]

            with nc.Block() as block:
                @block.gpsimd
                def _(pool):
                    pool.memset(acc[:, 0, :], 0.0)

                @block.vector
                def _(v):
                    v.memset(acc[:, 1, :], 0.0)

            with nc.Fori(0, passes):
                with nc.Block() as block:
                    @block.vector
                    def _(v):
                        v.sem_clear(tile_moved)
                        link = chained(v, tile_moved)
                        v.tensor_scalar(drel[:], drel[:], -float(WT), None, ALU.add)
                        link(v.tensor_scalar(prel0[:], prel0[:], float(WT), None, ALU.add))
                        v.tensor_scalar(prel[:], prel0[:], float(WC), None, ALU.add)
                        starts_c = starts[:, 1:, NGS:NGS + DPI]
                        v.tensor_scalar(starts_c, chunk_start0[:].rearrange("a (s c) -> a s c", c=DPI), -float(WC),
                                        None, ALU.add)
                        link(v.tensor_scalar(inside[:], drel[:], 0.0, None, ALU.is_ge))
                        link(v.scalar_tensor_tensor(out=inside[:], in0=drel[:], scalar=float(WT), in1=inside[:],
                                                    op0=ALU.is_lt, op1=ALU.mult))
                        link(v.scalar_tensor_tensor(out=key[:], in0=drel[:], scalar=1.0, in1=inside[:],
                                                    op0=ALU.add, op1=ALU.mult))
                        link(v.tensor_tensor(inside[:], inside[:], src_hi[:], ALU.mult))
                        v.scalar_tensor_tensor(out=key[:], in0=key[:], scalar=-1.0, in1=inside[:],
                                               op0=ALU.add, op1=ALU.add)
                with nc.Fori(0, chunk_passes):
                    with nc.Block() as block:
                        @block.vector
                        def _(v):
                            for s in per_pass:
                                v.sem_clear(s)
                            v.tensor_scalar(rel[:], rel[:], -float(W), None, ALU.add)
                            v.tensor_scalar(prel[:], prel[:], -float(WC), None, ALU.add)
                            v.tensor_scalar(starts[:, :, 0:NGS], starts[:, :, 0:NGS], float(W), None, ALU.add)
                            v.tensor_scalar(starts[:, 1:, NGS:NGS + DPI], starts[:, 1:, NGS:NGS + DPI], float(WC),
                                            None, ALU.add).then_inc(moved, 1)
                            v.wait_ge(moved, 1)
                            v.tensor_scalar(starts_int[:], starts[:], float(N), None, ALU.min)
                    with nc.Block() as block:
                        @block.sync
                        def _(sp):
                            def step(s):
                                for e, j in enumerate(ATTR):
                                    if e >= HOTS:
                                        sp.wait_ge(summed[ATTR[e - HOTS]], s + 1)
                                    else:
                                        need(sp, summed[ATTR[e - HOTS]], s)
                                    g = group_of(j, s)
                                    if not isinstance(s, int):
                                        rows_of = attr_groups[bass.ds(g, 1), :, :].rearrange("a p n -> p (a n)")
                                    else:
                                        rows_of = attr_groups[g, :, :] if g < FULL else attr_last
                                    sp.dma_start(attr[:, e % HOTS, :], rows_of).then_inc(attr_in[e % HOTS], 16)
                            step(0)
                            with sp.Fori(1, STEPS - 1) as s:
                                step(s)
                            step(STEPS - 1)

                        @block.gpsimd
                        def _(pool):
                            def step(s):
                                for k in range(NG1):
                                    pool.wait_ge(index_ready, s * NG1 + k + 1)
                                    need(pool, summed[GATH[k]], s)
                                    pool.sem_inc(gathers_open, 1)
                                    for t in range(GT):
                                        pool.indirect_dma_start(
                                            gathered[:, k, t, :], None, table,
                                            bass.IndirectOffsetOnAxis(ap=index[:, k, t:t + 1], axis=0),
                                        ).then_inc(gather_in[k], 16)
                            step(0)
                            with pool.Fori(1, STEPS) as s:
                                step(s)

                        @block.scalar
                        def _(act):
                            def next_index(s, k):
                                need(act, gather_in[k], s * 16 * GT)
                                g = src_t[:, bass.ds(s * NG1 + k, 1), :].rearrange("p a t -> p (a t)")
                                act.copy(index[:, k, :], g).then_inc(index_ready, 1)

                            def save_product(s, phase):
                                need(act, multiplied, s * DPI + phase - 1)
                                need(act, summed[CHNK[phase]], s - 1)
                                act.copy(product[:, phase, :], ps_product[phase][:, 0:2 * P]).then_inc(product_ready, 1)

                            def step(s):
                                for pair in range(DPI * CT // 2):
                                    phase, q = divmod(2 * pair, CT)
                                    act.wait_ge(built, s * DPI * CT + 2 * pair + 2)
                                    if q == 0:
                                        need(act, multiplied, s * DPI + phase - 1)
                                    act.copy(
                                        counts_sb[phase][:, :, q * WT:(q + 2) * WT].rearrange(
                                            "p h (t n) -> p t h n", n=WT),
                                        ps_counts[pair % 2][:, :, 0:KEYS].rearrange("p t (h n) -> p t h n", n=WT)
                                    ).then_inc(saved, 1)
                                    if q == 2 and not (isinstance(s, int) and s == 0):
                                        save_product(s, phase)
                                    for k, j in enumerate(GATH):
                                        if AT[j] // 2 + 1 == pair and not (isinstance(s, int) and s == STEPS - 1):
                                            next_index(s + 1, k)
                            for k in range(NG1):
                                next_index(0, k)
                            step(0)
                            step(1)
                            with act.Fori(2, STEPS - 1) as s:
                                step(s)
                            step(STEPS - 1)
                            for phase in range(DPI):
                                save_product(STEPS, phase)

                        @block.vector
                        def _(v):
                            regs = [v.alloc_register(f"start{k}") for k in range(NGS + DPI)]

                            def load_starts(s):
                                v.load(regs, starts_int[0:1, bass.ds(s, 1), 0:NGS + DPI].rearrange("a s g -> a (s g)"))

                            def chunk_item(s, j):
                                prev = prel[:, bass.ds(s * DPI + CHNK.index(j) - DPI, 1)]
                                v.tensor_scalar(chunk_hot[:], iota_c[:], prev, None, ALU.is_equal)\
                                 .then_inc(item_hot[j], 1)

                            def add_item(s, j, after):
                                for i, count in after:
                                    v.wait_ge(added[i], count)
                                v.wait_ge(summed[j], nth(j, s))
                                start = v.snap(regs[start_of(j)], min_val=0, max_val=N)
                                ps = ps_sums[j % 2]
                                if ITEMS[j] == "c":
                                    win, new = acc[:, 0, bass.ds(start, WC)], ps[:, 0:WC]
                                elif ITEMS[j] == "g":
                                    win = acc[:, :, bass.ds(start, W)]
                                    new = ps[:, 0:2 * W].rearrange("p (a n) -> p a n", a=2)
                                else:
                                    win, new = acc[:, 1, bass.ds(start, W)], ps[:, W:2 * W]
                                v.tensor_tensor(win, win, new, ALU.add).then_inc(added[j], 1)

                            def step(s):
                                zero = isinstance(s, int) and s == 0
                                load_starts(s)
                                for q in range(DPI * CT):
                                    need(v, built, s * DPI * CT + q + 1 - HOTS)
                                    tile = bass.ds(s * DPI * CT + q, 1)
                                    v.tensor_scalar(lo_hot[:, q % HOTS, :], iota_lo[:],
                                                    src_lo[:].rearrange("p g t -> p (g t)")[:, tile], None,
                                                    ALU.is_equal)
                                    v.tensor_scalar(key_hot[:, q % HOTS, :], iota_key[:],
                                                    key[:].rearrange("p g t -> p (g t)")[:, tile], None,
                                                    ALU.is_equal).then_inc(hot_ready, 1)
                                    if q in AT:
                                        j = AT.index(q)
                                        if not (zero and ITEMS[j] == "c"):
                                            for i, count in before(j, 2, s):
                                                v.wait_ge(summed[i], count)
                                            if ITEMS[j] == "c":
                                                chunk_item(s, j)
                                            else:
                                                group_hot(v, group_hots[:, j % 2], group_of(j, s), 1, iota_c[:, 0:W])\
                                                    .then_inc(item_hot[j], 1)
                                    if q - LAG in AT:
                                        j = AT.index(q - LAG)
                                        if not (zero and ITEMS[j] == "c"):
                                            add_item(s, j, before(j, 1, s))
                            step(0)
                            step(1)
                            with v.Fori(2, STEPS) as s:
                                step(s)
                            load_starts(STEPS)
                            last = NI - 1
                            v.wait_ge(summed[last], STEPS)
                            chunk_item(STEPS, CHNK[0])
                            add_item(STEPS, CHNK[0], [(last, STEPS)])
                            chunk_item(STEPS, CHNK[1])
                            add_item(STEPS, CHNK[1], [(CHNK[0], STEPS)])

                        @block.tensor
                        def _(pe):
                            def multiply(s, phase, blocks):
                                b = 1 - phase
                                if blocks[0] == 0:
                                    pe.wait_ge(saved, (s * DPI + phase) * (CT // 2))
                                    need(pe, product_ready, s * DPI + phase - 2)
                                for h in blocks:
                                    ins = pe.matmul(ps_product[b][:, 0:2 * P], counts_sb[b][:, h, :],
                                                    table_sb[:, h, :, :].rearrange("p a f -> p (a f)"),
                                                    start=(h == 0), stop=(h == NB - 1))
                                if blocks[-1] == NB - 1:
                                    ins.then_inc(multiplied, 1)

                            def sum_chunk(s, j):
                                phase = CHNK.index(j)
                                pe.wait_ge(product_ready, s * DPI + phase - 1)
                                pe.wait_ge(item_hot[j], nth(j, s))
                                for half in range(2):
                                    ins = pe.matmul(ps_sums[j % 2][:, 0:WC], product[:, phase, half * P:(half + 1) * P],
                                                    chunk_hot[:], start=(half == 0), stop=(half == 1))
                                ins.then_inc(summed[j], 1)

                            def sum_group(s, j):
                                e = ATTR.index(j)
                                ps = ps_sums[j % 2]
                                pe.wait_ge(item_hot[j], s + 1)
                                pe.wait_ge(attr_in[e % HOTS], 16 * (s * (len(ATTR) // HOTS) + e // HOTS + 1))
                                for t in range(GT):
                                    ins = pe.matmul(ps[:, W:2 * W], attr[:, e % HOTS, t * P:(t + 1) * P],
                                                    group_hots[:, j % 2, t, :], start=(t == 0), stop=(t == GT - 1))
                                if j in GATH:
                                    k = GATH.index(j)
                                    pe.wait_ge(gather_in[k], 16 * GT * (s + 1))
                                    for t in range(GT):
                                        ins = pe.matmul(ps[:, 0:W], gathered[:, k, t, :], group_hots[:, j % 2, t, :],
                                                        start=(t == 0), stop=(t == GT - 1))
                                ins.then_inc(summed[j], 1)

                            def step(s):
                                zero = isinstance(s, int) and s == 0
                                for q in range(DPI * CT):
                                    phase, slot = divmod(q, CT)
                                    if q % 2 == 0:
                                        need(pe, saved, s * (DPI * CT // 2) + q // 2 - 1)
                                    pe.wait_ge(hot_ready, s * DPI * CT + q + 1)
                                    pe.matmul(ps_counts[q // 2 % 2][:, q % 2, 0:KEYS], lo_hot[:, q % HOTS, :],
                                              key_hot[:, q % HOTS, :], start=True, stop=True).then_inc(built, 1)
                                    if slot in BLOCKS_AT and not (zero and phase == 0):
                                        multiply(s, phase, BLOCKS_AT[slot])
                                    if q in AT:
                                        j = AT.index(q)
                                        if zero and ITEMS[j] == "c":
                                            continue
                                        for i, count in before(j, 2, s):
                                            pe.wait_ge(added[i], count)
                                        if ITEMS[j] == "c":
                                            sum_chunk(s, j)
                                        else:
                                            sum_group(s, j)
                            step(0)
                            step(1)
                            with pe.Fori(2, STEPS) as s:
                                step(s)
                            multiply(STEPS, 0, range(NB))
                            for j in CHNK:
                                i = NI - 1 if j == CHNK[0] else CHNK[0]
                                pe.wait_ge(added[i], STEPS)
                                sum_chunk(STEPS, j)


        with ExitStack() as scope:
            def ring(name):
                return sb(name, [P, 2, NC], scope=scope)

            xs = sb("xs2", [P, NB, P], scope=scope)
            stats = sb("stats2", [P, NB, 6], scope=scope)
            self_ring, conv_ring, relu_ring, h2_ring, h2t_ring, z1_ring, z2_ring, y_ring = (
                ring(n) for n in ("self_ring", "conv_ring", "relu_ring", "h2_ring", "h2t_ring", "z1_ring", "z2_ring",
                                  "y_ring"))
            ps_turn, ps_1, ps_2, ps_3 = ([bank(f"ps_{n}{k}", [P, NC], scope) for k in range(2)]
                                         for n in ("t", "one", "two", "three"))
            (zeroed, self_ready, conv_turned, conv_ready, relu_ready, x1_ready, var_ok, root_ok, norm_ok, dve_step,
             h2_ready, h2_turned, h2t_ready, m1_ready, z1_ready, m2_ready, z2_ready, m3_ready, y_ready) = (
                sem(f"mlp_{n}", scope) for n in
                "zeroed self_ready conv_turned conv_ready relu_ready x1_ready var_ok root_ok norm_ok dve_step "
                "h2_ready h2_turned h2t_ready m1_ready z1_ready m2_ready z2_ready m3_ready y_ready".split())
            x_in = [sem(f"mlp_x_in{c}", scope) for c in range(CHUNKS)]
            y_out = [sem(f"y_out{k}", scope) for k in range(2)]

            def chunk(rows_of, c):
                return rows_of[:, c * BC:c * BC + width(c), :].rearrange("p b f -> p (b f)")

            def slot(buffers, c):
                return buffers[:, c % 2, 0:width(c) * P]

            with nc.Block() as block:
                @block.sync
                def _(sp):
                    for c in range(CHUNKS - 1):
                        sp.dma_start(xs[:, c * BC:(c + 1) * BC, :], x_full[:, c * BC:(c + 1) * BC, :])\
                          .then_inc(x_in[c], 16)
                    sp.wait_ge(zeroed, 1)
                    sp.dma_start(xs[0:TAILN, FB, :], x[FB * P:N, :]).then_inc(x_in[CHUNKS - 1], 16)
                    for c in range(CHUNKS):
                        sp.wait_ge(y_ready, c + 1)
                        rows_of = y_ring[:, c % 2, :].rearrange("p (b f) -> p b f", b=BC)
                        if c < CHUNKS - 1:
                            sp.dma_start(out_full[:, c * BC:(c + 1) * BC, :], rows_of).then_inc(y_out[c % 2], 16)
                        else:
                            sp.dma_start(out[FB * P:N, :], rows_of[0:TAILN, 0, :]).then_inc(y_out[c % 2], 16)
                    for k in range(2):
                        sp.wait_ge(y_out[k], 16 * ((CHUNKS - k + 1) // 2))

                @block.gpsimd
                def _(pool):
                    pool.memset(xs[:, FB, :], 0.0).then_inc(zeroed, 1)
                    for c in range(CHUNKS):
                        n = width(c)
                        if c >= 2:
                            pool.wait_ge(conv_ready, c - 1)
                        parts = table_sb[:, c * BC:c * BC + n, :, :].bitcast(F32)
                        pool.tensor_tensor(slot(self_ring, c).rearrange("p (b f) -> p b f", b=n), parts[:, :, 0, :],
                                           parts[:, :, 1, :], ALU.add).then_inc(self_ready, 1)

                @block.vector
                def _(v):
                    link = chained(v, dve_step)

                    def add_conv(c):
                        v.wait_ge(x_in[c], 16)
                        v.wait_ge(relu_ready, c + 1)
                        v.tensor_tensor(chunk(xs, c), slot(relu_ring, c), chunk(xs, c), ALU.add).then_inc(x1_ready, 1)
                        v.wait_ge(x1_ready, c + 1)
                        for b in range(c * BC, c * BC + width(c)):
                            ins = v.bn_stats(stats[:, b, :], xs[:, b, :])
                        return ins

                    for c in range(CHUNKS):
                        v.wait_ge(self_ready, c + 1)
                        v.wait_ge(conv_turned, c + 1)
                        if c >= 2:
                            v.wait_ge(relu_ready, c - 1)
                        v.tensor_tensor(slot(conv_ring, c), ps_turn[c % 2][:, 0:width(c) * P], slot(self_ring, c),
                                        ALU.add).then_inc(conv_ready, 1)
                        if c >= 1:
                            add_conv(c - 1)
                    link(add_conv(CHUNKS - 1))
                    layer_norm_stats(v, link, stats, var_ok, root_ok, norm_ok)

                    for s in range(CHUNKS + 3):
                        if s < CHUNKS:
                            v.wait_ge(h2_turned, s + 1)
                            if s >= 2:
                                v.wait_ge(m1_ready, s - 1)
                            v.tensor_copy(slot(h2t_ring, s), ps_turn[s % 2][:, 0:width(s) * P]).then_inc(h2t_ready, 1)
                        if s >= 3:
                            c = s - 3
                            v.wait_ge(m3_ready, c + 1)
                            if c >= 2:
                                v.wait_ge(y_out[c % 2], 16 * (c // 2))
                            v.tensor_tensor(slot(y_ring, c), ps_3[c % 2][:, 0:width(c) * P], chunk(xs, c), ALU.add)\
                             .then_inc(y_ready, 1)

                @block.scalar
                def _(act):
                    for c in range(CHUNKS):
                        act.wait_ge(conv_ready, c + 1)
                        if c >= 2:
                            act.wait_ge(x1_ready, c - 1)
                        for k in range(width(c)):
                            b = c * BC + k
                            part = slice(k * P, (k + 1) * P)
                            ins = act.activation(relu_ring[:, c % 2, part], conv_ring[:, c % 2, part], ACT.Relu,
                                                 scale=dinv[:, b:b + 1])
                        ins.then_inc(relu_ready, 1)
                    act.wait_ge(var_ok, 1)
                    act.activation(rstd[:], var[:], ACT.Sqrt, bias=eps_col[:]).then_inc(root_ok, 1)
                    act.wait_ge(norm_ok, 1)
                    for s in range(CHUNKS + 2):
                        if s < CHUNKS:
                            if s >= 2:
                                act.wait_ge(h2_turned, s - 1)
                            for k in range(width(s)):
                                n = s * BC + k
                                ins = act.activation(h2_ring[:, s % 2, k * P:(k + 1) * P], xs[:, n, :], ACT.Relu,
                                                     scale=rstd[:, n:n + 1], bias=shift[:, n:n + 1])
                            ins.then_inc(h2_ready, 1)
                        if 1 <= s <= CHUNKS:
                            c = s - 1
                            act.wait_ge(m1_ready, c + 1)
                            if c >= 2:
                                act.wait_ge(m2_ready, c - 1)
                            act.activation(slot(z1_ring, c), ps_1[c % 2][:, 0:width(c) * P], ACT.Relu, bias=b1u[:])\
                               .then_inc(z1_ready, 1)
                        if s >= 2:
                            c = s - 2
                            act.wait_ge(m2_ready, c + 1)
                            if c >= 2:
                                act.wait_ge(m3_ready, c - 1)
                            act.activation(slot(z2_ring, c), ps_2[c % 2][:, 0:width(c) * P], ACT.Relu, bias=B2)\
                               .then_inc(z2_ready, 1)

                @block.tensor
                def _(pe):
                    for c in range(CHUNKS):
                        if c >= 2:
                            pe.wait_ge(conv_ready, c - 1)
                        for k in range(width(c)):
                            b = c * BC + k
                            ins = pe.transpose(ps_turn[c % 2][:, k * P:(k + 1) * P], acc[:, 0, b * P:(b + 1) * P],
                                               ident[:])
                        ins.then_inc(conv_turned, 1)
                    pe.wait_ge(conv_ready, CHUNKS)
                    for s in range(CHUNKS + 3):
                        if s < CHUNKS:
                            pe.wait_ge(h2_ready, s + 1)
                            if s >= 2:
                                pe.wait_ge(h2t_ready, s - 1)
                            for k in range(width(s)):
                                part = slice(k * P, (k + 1) * P)
                                ins = pe.transpose(ps_turn[s % 2][:, part], h2_ring[:, s % 2, part], ident[:])
                            ins.then_inc(h2_turned, 1)
                        if 1 <= s <= CHUNKS:
                            c = s - 1
                            n = width(c) * P
                            pe.wait_ge(h2t_ready, c + 1)
                            if c >= 2:
                                pe.wait_ge(z1_ready, c - 1)
                            pe.matmul(ps_1[c % 2][:, 0:n], w1_sb[:, 0, :], slot(h2t_ring, c), start=True, stop=False)
                            pe.matmul(ps_1[c % 2][:, 0:n], w1_sb[:, 1, :], acc[:, 1, c * NC:c * NC + n],
                                      start=False, stop=True).then_inc(m1_ready, 1)
                        if 2 <= s <= CHUNKS + 1:
                            c = s - 2
                            pe.wait_ge(z1_ready, c + 1)
                            if c >= 2:
                                pe.wait_ge(z2_ready, c - 1)
                            pe.matmul(ps_2[c % 2][:, 0:width(c) * P], w2_sb[:], slot(z1_ring, c), start=True,
                                      stop=True).then_inc(m2_ready, 1)
                        if s >= 3:
                            c = s - 3
                            pe.wait_ge(z2_ready, c + 1)
                            if c >= 2:
                                pe.wait_ge(y_ready, c - 1)
                            for k in range(width(c)):
                                part = slice(k * P, (k + 1) * P)
                                pe.matmul(ps_3[c % 2][:, part], z2_ring[:, c % 2, part], w3_sb[:], start=True,
                                          stop=False)
                                ins = pe.matmul(ps_3[c % 2][:, part], ones_row[:], b3_row[:], start=False, stop=True)
                            ins.then_inc(m3_ready, 1)


_INS = ['x', 'src', 'dst', 'edge_attr_128', 'L0_gnn_W', 'L0_gnn_b', 'L0_gnn_gamma', 'L0_gnn_beta', 'L1_gnn_u',
        'L1_gnn_W1', 'L1_gnn_b1', 'L1_gnn_W2', 'L1_gnn_b2', 'L1_gnn_W3', 'L1_gnn_b3']
_OUTS = [((6250, 128), 'float32')]


def kernel(**inputs):
    import numpy as _np
    import concourse.bacc as _bacc
    from concourse import mybir as _mybir
    from concourse.bass_utils import run_bass_kernel_spmd as _run

    nc = _bacc.Bacc("TRN2", target_bir_lowering=False, num_devices=1)
    arrays, args = {}, []
    for name in _INS:
        a = _np.ascontiguousarray(inputs[name])
        arrays[f"in_{name}_dram"] = a
        args.append(nc.dram_tensor(f"in_{name}_dram", a.shape, _mybir.dt.from_np(a.dtype), kind="ExternalInput").ap())
    for i, (shape, dtype) in enumerate(_OUTS):
        dt = _mybir.dt.from_np(_np.dtype(dtype))
        args.append(nc.dram_tensor(f"out_{i}_dram", shape, dt, kind="ExternalOutput").ap())
    gnn_kernel(nc, *args)
    r = _run(nc, [arrays], core_ids=[0])
    got = tuple(r.results[0][f"out_{i}_dram"] for i in range(len(_OUTS)))
    return got[0]
```

```python
from contextlib import ExitStack

import concourse.bass as bass
from concourse import mybir

F32 = mybir.dt.float32
F32R = mybir.dt.float32r
BF16 = mybir.dt.bfloat16
F16 = mybir.dt.float16
I32 = mybir.dt.int32
ALU = mybir.AluOpType
ACT = mybir.ActivationFunctionType
AX = mybir.AxisListType

P = 128
TILE = 128
GT = 4
W = 24
WT = 6
CG = 5
CT = CG * GT
CP = CG * W
WC = 96
DPI = 2
NG1 = 8
NG2 = DPI * CG
NGS = NG1 + NG2
HOTS = 4
ATTRS = 6
GATHERS = 4
EPS = 1e-5
TABLE = F16
NOWHERE = 1.0e6
FAR = NOWHERE / 4


def gnn_kernel(nc, x, src, dst, edge_attr, w_gcn, b_gcn, gamma, beta, u, w1, b1, w2, b2, w3, b3, out):
    N, D = x.shape
    E = src.shape[0]
    assert D == P and WT * CT == CP <= P
    NC = 512
    BC = NC // P
    NB = -(-N // P)
    CHUNKS = -(-NB // BC)
    FB = N // P
    TAILN = N - FB * P
    GE = GT * TILE
    FULL = E // GE
    OVER = (FULL + 1) * GE - E
    STEPS = -(-(FULL + 1) // NGS)
    NG = STEPS * NGS
    GG = STEPS * NG1
    DG = NG - GG
    DCH = DG // CG
    DT = DG * GT
    COUNTED = 9 * CG
    DS = -(-(FULL + 1) // COUNTED)
    NGP = -(-max(NG, DS * COUNTED) // CG) * CG
    FIVES = NGP // CG
    RC = -(-NG // P)
    RD = GG // P
    AW = N + WC
    KEYS = NB * WT
    assert E % GE and FB == NB - 1 == (CHUNKS - 1) * BC and AW >= NB * P and NB <= P
    assert 3 * RC * GE <= NB * P and RC * P <= 512 and KEYS <= 512
    assert NGS % ATTRS == 0 and NG1 % GATHERS == 0

    def width(c):
        return min(BC, NB - c * BC)

    table = nc.dram_tensor("scaled_h_table", (NB * P, P), F32, kind="Internal").ap()
    src_rows = src[0:FULL * GE].rearrange("(g e) -> g e", e=GE)
    dst_rows = dst[0:FULL * GE].rearrange("(g e) -> g e", e=GE)
    src_last = src[E - GE:E].rearrange("(a e) -> a e", a=1)
    dst_last = dst[E - GE:E].rearrange("(a e) -> a e", a=1)
    attr_groups = edge_attr[0:FULL * GE, :].rearrange("(g p t) f -> g p (t f)", p=P, t=GT)
    attr_last = edge_attr[E - GE:E, :].rearrange("(p t) f -> p (t f)", t=GT)
    x_full = x[0:FB * P, :].rearrange("(b p) f -> p b f", p=P)
    table_blocks = table.rearrange("(b p) f -> p b f", p=P)
    out_full = out[0:FB * P, :].rearrange("(b p) f -> p b f", p=P)

    with ExitStack() as ctx:
        def sb(name, shape, dt=F32, scope=ctx):
            return scope.enter_context(nc.sbuf_tensor(name, shape, dt))

        def bank(name, shape, scope):
            return scope.enter_context(nc.psum_tensor(name, shape, F32))

        def sem(name, scope):
            return scope.enter_context(nc.semaphore(name))

        def chained(v, steps):
            count = [0]

            def link(ins):
                count[0] += 1
                ins.then_inc(steps, 1)
                v.wait_ge(steps, count[0])
            return link

        dinv = sb("dinv", [P, NB])
        table_sb = sb("table_sb", [P, NB, 2, P], F32R)
        acc = sb("acc", [P, 2, AW])
        mean = sb("mean", [P, NB])
        var = sb("var", [P, NB])
        rstd = sb("rstd", [P, NB])
        shift = sb("shift", [P, NB])
        rel = sb("rel", [P, NGP, GT])
        src_t = sb("src_t", [P, GG, GT])
        drel = sb("drel", [P, DG, GT])
        src_lo = sb("src_lo", [P, DG, GT], TABLE)
        src_hi = sb("src_hi", [P, DG, GT], F16)
        key = sb("key", [P, DG, GT], TABLE)
        inside = sb("inside", [P, DG, GT], F16)
        prel0 = sb("prel0", [CP, DCH])
        prel = sb("prel", [CP, DCH])
        window_node = sb("window_node", [CP, FIVES])
        starts = sb("starts", [1, STEPS + 1, NGS + DPI])
        starts_int = sb("starts_int", [1, STEPS + 1, NGS + DPI], I32)
        chunk_start0 = sb("chunk_start0", [1, DCH])
        span_int = sb("span_int", [1, 2], I32)
        iota_c = sb("iota_c", [P, WC])
        iota_lo = sb("iota_lo", [P, P], F16)
        iota_key = sb("iota_key", [P, KEYS], F16)
        ident = sb("ident", [P, P])
        ones_row = sb("ones_row", [1, P])
        ones_col = sb("ones_col", [P, 1], BF16)
        eps_col = sb("eps_col", [P, 1])
        w1_sb = sb("w1_sb", [P, 3, P])
        w2_sb = sb("w2_sb", [P, P])
        w3_sb = sb("w3_sb", [P, P])
        cols = sb("cols", [P, 6])
        B_GCN, GAMMA, BETA, B1, B2, U = (cols[:, k:k + 1] for k in range(6))
        b1u = sb("b1u", [P, 1])
        bn = sb("bn", [P, 8])

        def layer_norm_stats(v, link, stats, var_ready, root_ready, norm_ready):
            m0, m1, s0, s1 = stats[:, :, 1], stats[:, :, 4], stats[:, :, 2], stats[:, :, 5]
            v.tensor_tensor(mean[:], m0, m1, ALU.add)
            v.tensor_tensor(shift[:], m0, m1, ALU.subtract)
            link(v.tensor_tensor(rstd[:], s0, s1, ALU.add))
            v.tensor_scalar(mean[:], mean[:], 0.5, None, ALU.mult)
            link(v.scalar_tensor_tensor(out=shift[:], in0=shift[:], scalar=0.25, in1=shift[:],
                                        op0=ALU.mult, op1=ALU.mult))
            v.scalar_tensor_tensor(out=var[:], in0=rstd[:], scalar=1.0 / P, in1=shift[:],
                                   op0=ALU.mult, op1=ALU.add).then_inc(var_ready, 1)
            v.wait_ge(root_ready, 1)
            link(v.reciprocal(rstd[:], rstd[:]))
            v.scalar_tensor_tensor(out=shift[:], in0=mean[:], scalar=-1.0, in1=rstd[:],
                                   op0=ALU.mult, op1=ALU.mult).then_inc(norm_ready, 1)

        early = ExitStack()
        h_t = sb("h_t", [P, NB * P], scope=early)

        linear = ExitStack()
        space = acc[:].rearrange("p a n -> p (a n)")
        xs = space[:, 0:NB * P].rearrange("p (b f) -> p b f", f=P)
        wg_t = sb("wg_t", [P, P], scope=linear)
        h_ring = sb("h_ring", [P, 2, BC, P], scope=linear)
        ht_ring = sb("ht_ring", [P, 2, NC], scope=linear)
        sums = sb("sums", [P, 2, CHUNKS + 1], scope=linear)

        with ExitStack() as scope:
            raw, edge_f, unmasked = (space[:, NB * P + k * RC * GE:NB * P + (k + 1) * RC * GE]
                                     .rearrange("p (c e) -> p c e", c=RC) for k in range(3))
            raw = raw.bitcast(I32)
            raw_last = sb("raw_last", [1, GE], I32, scope)
            last_f = sb("last_f", [1, GE], scope=scope)
            tile_min = sb("tile_min", [P, RC, GT], scope=scope)
            tile_max = sb("tile_max", [P, RC, GT], scope=scope)
            group_lim = sb("group_lim", [P, 2, RC], scope=scope)
            spans = sb("spans", [P, 2, RC * GT], scope=scope)
            span_cols = sb("span_cols", [P, 2], scope=scope)
            span_row = sb("span_row", [1, 8], scope=scope)
            group_rows = sb("group_rows", [1, 2, NGP], scope=scope)
            chunk_max = sb("chunk_max", [1, DCH], scope=scope)
            chunk_min = sb("chunk_min", [1, DCH], scope=scope)
            tile_row = sb("tile_row", [1, DG, GT], scope=scope)
            band = sb("band", [1, 2 * P], scope=scope)
            nodes_row = sb("nodes_row", [1, CP], scope=scope)
            wide_band = sb("wide_band", [1, 2 * P], scope=scope)
            wide_nodes_row = sb("wide_nodes_row", [1, CP], scope=scope)
            minus_start = sb("minus_start", [1, DCH], scope=scope)
            lo_int = sb("lo_int", [P, DG, GT], I32, scope)
            hi_int = sb("hi_int", [P, DG, GT], I32, scope)
            stats = sb("stats", [P, NB, 6], scope=scope)
            w_raw = sb("w_raw", [P, P], scope=scope)
            turn = [bank(f"turn{k}", [P, GT, P], scope) for k in range(2)]
            ps_turn = [bank(f"ps_turn{k}", [P, BC, P], scope) for k in range(2)]
            ps_lin = [bank(f"ps_lin{k}", [P, NC], scope) for k in range(2)]
            ps_row = bank("ps_row", [P, 512], scope)
            ps_small = bank("ps_small", [P, 512], scope)

            (x_in, dst_in, src_in, last_in, w_in, dst_cast, src_cast, last_put, zeroed, ident_ok, consts, turned,
             dst_read, src_read, limits, rows_t, spread, spread_read, dve_step, var_ok, root_ok, norm_ok,
             w_turned, wg_ready, b1u_done, stats_done) = (sem(n, scope) for n in
                  "x_in dst_in src_in last_in w_in dst_cast src_cast last_put zeroed ident_ok consts turned "
                  "dst_read src_read limits rows_t spread spread_read ln_step var_ok root_ok norm_ok "
                  "w_turned wg_ready b1u_done stats_done".split())
            W_LOADS = 10
            CONSTS = 8

            def rows(c):
                return min(P, FULL + 1 - c * P)

            turns = [("dst", c, True) for c in range(RC)] + [("dst", c, False) for c in range(RD, RC)]
            DST_TURNS = len(turns)
            turns += [("src", c, True) for c in range(RD + 1)] + [("src", c, False) for c in range(RD, RC)]

            def dense_part(c):
                first = max(0, GG - c * P)
                return first, c * P + first - GG

            with nc.Block() as block:
                @block.sync
                def _(sp):
                    last = FULL - (RC - 1) * P

                    def load_rows(view, arrived):
                        for c in range(RC):
                            n = min(P, FULL - c * P)
                            sp.dma_start(raw[0:n, c, :], view[c * P:c * P + n, :]).then_inc(arrived, 16)

                    load_rows(dst_rows, dst_in)
                    sp.dma_start(raw_last[:], dst_last).then_inc(last_in, 16)
                    sp.dma_start(xs[:, 0:FB, :], x_full).then_inc(x_in, 16)
                    sp.wait_ge(zeroed, 1)
                    sp.dma_start(xs[0:TAILN, FB, :], x[FB * P:N, :]).then_inc(x_in, 16)
                    sp.dma_start(w_raw[:], w_gcn).then_inc(w_in, 16)
                    for k, vec in enumerate((b_gcn, gamma, beta, b1, b2)):
                        sp.dma_start(cols[:, k:k + 1], vec.rearrange("(p a) -> p a", a=1)).then_inc(w_in, 16)
                    sp.dma_start(U, u[0:1, :].rearrange("a p -> p a")).then_inc(w_in, 16)
                    sp.dma_start(w1_sb[:], w1.rearrange("(k p) n -> p k n", p=P)).then_inc(w_in, 16)
                    sp.dma_start(w2_sb[:], w2).then_inc(w_in, 16)
                    sp.dma_start(w3_sb[:], w3).then_inc(w_in, 16)
                    sp.wait_ge(dst_cast, 2)
                    sp.dma_start(edge_f[last:last + 1, RC - 1, :], last_f[:]).then_inc(last_put, 16)
                    load_rows(src_rows, src_in)
                    sp.dma_start(raw[last:last + 1, RC - 1, :], src_last).then_inc(src_in, 16)
                    sp.wait_ge(last_put, 16)
                    sp.wait_ge(src_in, 16 * (RC + 1))

                @block.gpsimd
                def _(pool):
                    pool.memset(xs[:, FB:NB, :], 0.0).then_inc(zeroed, 1)
                    pool.memset(ident[:], 0.0).then_inc(consts, 1)
                    pool.wait_ge(consts, 1)
                    pool.affine_select(out=ident[:], in_=ident[:], compare_op=ALU.not_equal, fill=1.0, base=0,
                                       pattern=[[-1, P]], channel_multiplier=1).then_inc(ident_ok, 1)
                    for target, pattern in ((iota_c, [[1, WC]]), (iota_lo, [[1, P]]), (iota_key, [[1, KEYS]]),
                                            (nodes_row, [[0, CT], [1, WT]]), (wide_nodes_row, [[0, CG], [1, W]])):
                        pool.iota(target[:], pattern, base=0, channel_multiplier=0,
                                  allow_small_or_imprecise_dtypes=True).then_inc(consts, 1)
                    pool.memset(ones_row[:], 1.0).then_inc(consts, 1)
                    pool.memset(ones_col[:], 1.0).then_inc(consts, 1)
                    pool.wait_ge(consts, CONSTS)

                @block.vector
                def _(v):
                    link = chained(v, dve_step)
                    v.memset(tile_min[:], FAR)
                    v.memset(tile_max[:], 0.0)
                    v.memset(group_rows[:, 0, :], FAR)
                    v.memset(group_rows[:, 1, :], 0.0)
                    v.memset(tile_row[:], FAR)
                    v.memset(span_cols[:], 0.0)
                    v.memset(starts[:], 0.0)
                    v.memset(rel[:], NOWHERE)
                    v.memset(drel[:], NOWHERE)
                    v.memset(lo_int[:], 0)
                    v.memset(band[:], 0.0)
                    v.memset(wide_band[:], 0.0)
                    link(v.memset(eps_col[:], EPS))
                    v.memset(band[:, P:P + WT], 1.0)
                    v.memset(wide_band[:, P:P + W], 1.0)
                    v.wait_ge(last_in, 16)
                    link(v.tensor_copy(last_f[:], raw_last[:]))
                    v.memset(last_f[:, 0:OVER], NOWHERE).then_inc(dst_cast, 1)
                    v.wait_ge(dst_in, 16 * RC)
                    for c in range(RC):
                        n = min(P, FULL - c * P)
                        ins = v.tensor_copy(edge_f[0:n, c, :], raw[0:n, c, :])
                    ins.then_inc(dst_cast, 1)
                    v.wait_ge(dst_cast, 2)
                    v.wait_ge(last_put, 16)
                    for c in range(RC):
                        r = rows(c)
                        v.tensor_reduce(tile_min[0:r, c, :], edge_f[0:r, c, :].rearrange("g (t e) -> g t e", t=GT),
                                        AX.X, ALU.min)
                        ins = v.scalar_tensor_tensor(out=unmasked[0:r, c, :], in0=edge_f[0:r, c, :],
                                                     scalar=NOWHERE / 2, in1=edge_f[0:r, c, :],
                                                     op0=ALU.is_lt, op1=ALU.mult)
                    link(ins)
                    for c in range(RC):
                        r = rows(c)
                        ins = v.tensor_reduce(tile_max[0:r, c, :],
                                              unmasked[0:r, c, :].rearrange("g (t e) -> g t e", t=GT), AX.X, ALU.max)
                    link(ins)
                    v.tensor_reduce(group_lim[:, 0, :], tile_min[:], AX.X, ALU.min)
                    v.tensor_reduce(group_lim[:, 1, :], tile_max[:], AX.X, ALU.max)
                    link(v.tensor_tensor(spans[:, 0, :], tile_max[:].rearrange("p c t -> p (c t)"),
                                         tile_min[:].rearrange("p c t -> p (c t)"), ALU.subtract))
                    link(v.tensor_tensor(spans[:, 1, 0:RC], group_lim[:, 1, :], group_lim[:, 0, :], ALU.subtract))
                    v.tensor_reduce(span_cols[:, 0:1], spans[:, 0, :], AX.X, ALU.max)
                    v.tensor_reduce(span_cols[:, 1:2], spans[:, 1, 0:RC], AX.X, ALU.max).then_inc(limits, 1)

                    def save_dst(t):
                        _, c, grouped = turns[t]
                        v.wait_ge(turned, t + 1)
                        if grouped:
                            target, first = rel[:, c * P:c * P + rows(c), :], 0
                        else:
                            first, place = dense_part(c)
                            target = drel[:, place:place + rows(c) - first, :]
                        v.tensor_copy(target.rearrange("p g t -> p t g"), turn[t % 2][:, :, first:rows(c)])\
                         .then_inc(dst_read, 1)

                    for t in range(DST_TURNS):
                        save_dst(t)
                    v.wait_ge(rows_t, 1)
                    for c in range(RC):
                        v.tensor_copy(group_rows[:, 0, c * P:c * P + rows(c)], ps_row[0:1, c * P:c * P + rows(c)])
                    v.wait_ge(rows_t, 2)
                    for c in range(RC):
                        v.tensor_copy(group_rows[:, 1, c * P:c * P + rows(c)], ps_small[0:1, c * P:c * P + rows(c)])
                    v.wait_ge(rows_t, 3)
                    v.tensor_reduce(span_row[:, 0:1], ps_lin[0][0:1, 0:P], AX.X, ALU.max)
                    link(v.tensor_reduce(span_row[:, 1:2], ps_lin[0][0:1, P:2 * P], AX.X, ALU.max))
                    ps_tiles = {RD: ps_lin[1], RD + 1: ps_turn[0], RD + 2: ps_turn[1]}
                    for c in range(RD, RC):
                        v.wait_ge(rows_t, 4 + c - RD)
                        first, place = dense_part(c)
                        ps = ps_tiles[c]
                        ps = ps[:].rearrange("p b n -> p (b n)") if c > RD else ps[:]
                        ins = v.tensor_copy(
                            tile_row[:, place:place + rows(c) - first, :].rearrange("a g t -> a t g"),
                            ps[0:1, :].rearrange("a (t g) -> a t g", t=GT)[:, :, first:rows(c)])
                    link(ins)
                    v.tensor_reduce(chunk_min[:], group_rows[:, 0, GG:NG].rearrange("a (c g) -> a c g", g=CG),
                                    AX.X, ALU.min)
                    link(v.tensor_reduce(chunk_max[:], group_rows[:, 1, GG:NG].rearrange("a (c g) -> a c g", g=CG),
                                         AX.X, ALU.max))
                    link(v.tensor_tensor(chunk_max[:], chunk_max[:], chunk_min[:], ALU.subtract))
                    v.tensor_scalar(minus_start[:], chunk_min[:], -1.0, None, ALU.mult)
                    v.tensor_copy(chunk_start0[:], chunk_min[:])
                    link(v.tensor_reduce(span_row[:, 2:3], chunk_max[:], AX.X, ALU.max))
                    link(v.tensor_scalar(span_row[:, 3:4], span_row[:, 0:1], float(W // WT), None, ALU.mult))
                    link(v.tensor_tensor(span_row[:, 1:2], span_row[:, 1:2], span_row[:, 3:4], ALU.max))
                    link(v.tensor_scalar(span_row[:, 1:3], span_row[:, 1:3], 0.0, None, ALU.max))
                    v.tensor_copy(span_int[:], span_row[:, 1:3])
                    v.tensor_scalar(starts[:, 0:STEPS, 0:NG1],
                                    group_rows[:, 0, 0:GG].rearrange("a (s g) -> a s g", g=NG1), -float(W), None,
                                    ALU.add)
                    v.tensor_scalar(starts[:, 0:STEPS, NG1:NGS],
                                    group_rows[:, 0, GG:NG].rearrange("a (s g) -> a s g", g=NG2), -float(W), None,
                                    ALU.add).then_inc(limits, 1)
                    v.wait_ge(spread, 1)
                    link(v.tensor_tensor(rel[:], rel[:], ps_row[:, 0:NGP].unsqueeze(2).to_broadcast([P, NGP, GT]),
                                         ALU.subtract))
                    v.tensor_scalar(rel[:], rel[:], float(W), None, ALU.add)
                    flat = drel[:].rearrange("p g t -> p (g t)")
                    SPREADS = -(-DT // 512)
                    for k in range(SPREADS):
                        n = slice(k * 512, min(DT, (k + 1) * 512))
                        v.wait_ge(spread, 2 + k)
                        ins = v.tensor_tensor(flat[:, n], flat[:, n], turn[k % 2][:].rearrange("p t n -> p (t n)")
                                              [:, 0:n.stop - n.start], ALU.subtract)
                        ins.then_inc(spread_read, 1)
                    v.wait_ge(spread_read, SPREADS)
                    v.tensor_scalar(drel[:], drel[:], float(WT), None, ALU.add)
                    v.wait_ge(x_in, 32)
                    for b in range(NB):
                        ln_stats = v.bn_stats(stats[:, b, :], xs[:, b, :])
                    ln_stats.then_inc(stats_done, 1)
                    v.wait_ge(spread, 2 + SPREADS)
                    v.tensor_scalar(prel0[:], ps_small[0:CP, 0:DCH], -float(WT), None, ALU.add)
                    v.tensor_scalar(window_node[:], ps_small[0:CP, 256:256 + FIVES], -float(W), None, ALU.add)\
                     .then_inc(spread_read, 1)
                    v.wait_ge(w_turned, 1)
                    v.tensor_copy(wg_t[:], ps_small[:, 128:256]).then_inc(wg_ready, 1)

                    v.wait_ge(stats_done, 1)
                    layer_norm_stats(v, link, stats, var_ok, root_ok, norm_ok)

                    v.wait_ge(src_read, len(turns) - DST_TURNS)
                    link(v.tensor_single_scalar(hi_int[:], lo_int[:], 7, ALU.logical_shift_right))
                    link(v.tensor_single_scalar(lo_int[:], lo_int[:], P - 1, ALU.bitwise_and))
                    v.tensor_copy(src_lo[:], lo_int[:])
                    v.tensor_scalar(src_hi[:], hi_int[:], float(WT), None, ALU.mult)

                    v.wait_ge(b1u_done, 1)
                    v.tensor_tensor(b1u[:], ps_small[:, 448:449], B1, ALU.add)

                @block.scalar
                def _(act):
                    act.wait_ge(src_in, 16 * (RC + 1))
                    act.wait_ge(turned, DST_TURNS)
                    act.wait_ge(limits, 1)
                    for c in range(RC):
                        ins = act.copy(edge_f[0:rows(c), c, :], raw[0:rows(c), c, :])
                    ins.then_inc(src_cast, 1)
                    for t in range(DST_TURNS, len(turns)):
                        _, c, grouped = turns[t]
                        act.wait_ge(turned, t + 1)
                        if grouped:
                            n = min(P, GG - c * P)
                            first, target = 0, src_t[:, c * P:c * P + n, :]
                        else:
                            first, place = dense_part(c)
                            n = rows(c)
                            target = lo_int[:, place:place + n - first, :]
                        act.copy(target.rearrange("p g t -> p t g"), turn[t % 2][:, :, first:n]).then_inc(src_read, 1)
                    act.wait_ge(var_ok, 1)
                    act.activation(rstd[:], var[:], ACT.Sqrt, bias=eps_col[:]).then_inc(root_ok, 1)
                @block.tensor
                def _(pe):
                    def turn_rows(t):
                        _, c, grouped = turns[t]
                        if t >= 2:
                            pe.wait_ge(*((dst_read, t - 1) if t - 2 < DST_TURNS else (src_read, t - 1 - DST_TURNS)))
                        r = rows(c)
                        order = "g (p t) -> g t p" if grouped else "g (t p) -> g t p"
                        for j in range(GT):
                            ins = pe.transpose(turn[t % 2][:, j, 0:r],
                                               edge_f[0:r, c, :].rearrange(order, t=GT)[:, j, :], ident[0:r, 0:r])
                        ins.then_inc(turned, 1)

                    pe.wait_ge(ident_ok, 1)
                    pe.wait_ge(dst_cast, 2)
                    pe.wait_ge(last_put, 16)
                    for t in range(DST_TURNS):
                        turn_rows(t)
                    pe.wait_ge(limits, 1)
                    for m, ps in ((0, ps_row), (1, ps_small)):
                        for c in range(RC):
                            ins = pe.transpose(ps[0:1, c * P:(c + 1) * P], group_lim[:, m, c:c + 1], ident[:])
                        ins.then_inc(rows_t, 1)
                    for m in range(2):
                        ins = pe.transpose(ps_lin[0][0:1, m * P:(m + 1) * P], span_cols[:, m:m + 1], ident[:])
                    ins.then_inc(rows_t, 1)
                    ps_tiles = {RD: ps_lin[1], RD + 1: ps_turn[0], RD + 2: ps_turn[1]}
                    for c in range(RD, RC):
                        ps = ps_tiles[c]
                        ps = ps[:].rearrange("p b n -> p (b n)") if c > RD else ps[:]
                        for t in range(GT):
                            ins = pe.transpose(ps[0:1, t * P:(t + 1) * P], tile_min[:, c, t:t + 1], ident[:])
                        ins.then_inc(rows_t, 1)
                    pe.wait_ge(consts, CONSTS)
                    pe.wait_ge(limits, 2)
                    pe.matmul(ps_row[:, 0:NGP], ones_row[:], group_rows[:, 0, :], start=True, stop=True)\
                      .then_inc(spread, 1)
                    tiles = tile_row[:].rearrange("a g t -> a (g t)")
                    for k in range(-(-DT // 512)):
                        n = slice(k * 512, min(DT, (k + 1) * 512))
                        if k >= 2:
                            pe.wait_ge(spread_read, k - 1)
                        else:
                            pe.wait_ge(dst_read, DST_TURNS)
                        pe.matmul(turn[k % 2][:].rearrange("p t n -> p (t n)")[:, 0:n.stop - n.start], ones_row[:],
                                  tiles[:, n], start=True, stop=True).then_inc(spread, 1)
                    for g in range(CG):
                        pe.matmul(ps_small[0:CP, 256:256 + FIVES], wide_band[:, P - W * g:P - W * g + CP],
                                  group_rows[:, 0, :].rearrange("a (q g) -> a g q", g=CG)[:, g, :],
                                  start=(g == 0), stop=False)
                    pe.matmul(ps_small[0:CP, 256:256 + FIVES], wide_nodes_row[:], ones_row[:, 0:FIVES], start=False,
                              stop=True)
                    for t in range(CT):
                        pe.matmul(ps_small[0:CP, 0:DCH], band[:, P - WT * t:P - WT * t + CP],
                                  tiles.rearrange("a (c t) -> a t c", t=CT)[:, t, :], start=(t == 0), stop=False)
                    pe.matmul(ps_small[0:CP, 0:DCH], ones_row[:, 0:CP], minus_start[:], start=False, stop=False)
                    pe.matmul(ps_small[0:CP, 0:DCH], nodes_row[:], ones_row[:, 0:DCH], start=False, stop=True)\
                      .then_inc(spread, 1)
                    pe.wait_ge(w_in, 16 * W_LOADS)
                    pe.wait_ge(spread_read, -(-DT // 512) + 1)
                    pe.transpose(ps_small[:, 128:256], w_raw[:], ident[:]).then_inc(w_turned, 1)
                    pe.wait_ge(src_cast, 1)
                    for t in range(DST_TURNS, len(turns)):
                        turn_rows(t)
                    pe.wait_ge(wg_ready, 1)
                    pe.matmul(ps_small[:, 448:449], w1_sb[:, 2, :], U, start=True, stop=True).then_inc(b1u_done, 1)

        span = nc.values_load(span_int[0:1, 0:1], min_val=0, max_val=N * (W // WT))
        chunk_span = nc.values_load(span_int[0:1, 1:2], min_val=0, max_val=N)
        passes = nc.snap(span // W + 1)
        chunk_passes = nc.snap(chunk_span // WC + 1)

        def group_hot(v, target, g, count, node_type_iota):
            offsets = rel[:, bass.ds(g, count), :].rearrange("p g t -> p (g t)")
            return v.tensor_tensor(target, offsets.unsqueeze(2).to_broadcast([P, count * GT, W]),
                                   node_type_iota.unsqueeze(1).to_broadcast([P, count * GT, W]), ALU.is_equal)

        with ExitStack() as scope:
            QS = COUNTED // CG
            hot = [sb(f"deg_hot{k}", [P, GT, COUNTED, W], BF16, scope) for k in range(2)]
            low_hot = sb("low_hot", [CP, 2, QS, P], F16, scope)
            block_hot = sb("block_hot", [CP, 2, QS, NB], F16, scope)
            step_block = sb("step_block", [CP, 2, QS], scope=scope)
            tally = sb("tally", [CP, 2, QS], scope=scope)
            node_int = sb("node_int", [CP, 2, FIVES], I32, scope)
            node_low = sb("node_low", [CP, FIVES], scope=scope)
            node_block = sb("node_block", [CP, FIVES], scope=scope)
            ps_tally = [bank(f"ps_tally{k}", [P, 512], scope) for k in range(2)]
            ps_degree = bank("ps_degree", [P, 512], scope)
            ps_turn = [bank(f"ps_h{k}", [P, NC], scope) for k in range(2)]
            ps_lin = [bank(f"ps_linear{k}", [P, NC], scope) for k in range(2)]
            hot_ready, counted, tallied, low_made, weighed, placed, weigh_open, deg_step = (
                sem(f"deg_{n}", scope) for n in
                "hot counted tallied low_made weighed placed weigh_open step".split())
            h_ready, h_turned, ht_ready, lin_ready, lin_saved, bn_step = (
                sem(f"lin_{n}", scope) for n in ("h_ready", "h_turned", "ht_ready", "lin_ready", "saved", "step"))
            with nc.Block() as block:
                @block.vector
                def _(v):
                    v.memset(dinv[:], 0.0)
            def degree_pass(with_linear):
                with nc.Block() as block:
                    @block.vector
                    def _(v):
                        for s in (hot_ready, counted, tallied, low_made, weighed, placed, weigh_open, deg_step):
                            v.sem_clear(s)
                        link = chained(v, deg_step)
                        v.tensor_scalar(rel[:], rel[:], -float(W), None, ALU.add)
                        link(v.tensor_scalar(window_node[:], window_node[:], float(W), None, ALU.add))
                        link(v.tensor_copy(node_int[:, 0, :], window_node[:]))
                        v.tensor_single_scalar(node_int[:, 1, :], node_int[:, 0, :], 7, ALU.logical_shift_right)
                        link(v.tensor_single_scalar(node_int[:, 0, :], node_int[:, 0, :], P - 1, ALU.bitwise_and))
                        v.tensor_copy(node_low[:], node_int[:, 0, :])
                        v.tensor_copy(node_block[:], node_int[:, 1, :])
                with nc.Block() as block:
                    @block.vector
                    def _(v):
                        def make_hot(s, b, reuse):
                            if reuse:
                                v.wait_ge(counted, s - 1)
                            whole = [P, COUNTED, GT, W]
                            offsets = rel[:, bass.ds(s * COUNTED, COUNTED), :]
                            v.tensor_tensor(hot[b][:].rearrange("p t g n -> p g t n"),
                                            offsets.unsqueeze(3).to_broadcast(whole),
                                            iota_c[:, 0:W].unsqueeze(1).unsqueeze(1).to_broadcast(whole),
                                            ALU.is_equal).then_inc(hot_ready, 1)

                        def weigh(s, b, reuse):
                            v.wait_ge(counted, s + 1)
                            if reuse:
                                v.wait_ge(placed, s - 1)
                            v.tensor_copy(step_block[:, b, :], node_block[:, bass.ds(s * QS, QS)])
                            v.tensor_copy(tally[:, b, :], ps_tally[b][0:CP, 0:QS]).then_inc(tallied, 1)
                            v.wait_ge(tallied, s + 1)
                            for k in range(QS):
                                five = bass.ds(s * QS + k, 1)
                                ins = v.tensor_scalar(low_hot[:, b, k, :], iota_lo[0:CP, :], node_low[:, five], None,
                                                      ALU.is_equal)
                            ins.then_inc(low_made, 1)

                        make_hot(0, 0, False)
                        make_hot(1, 1, False)
                        weigh(0, 0, False)
                        make_hot(2, 0, True)
                        weigh(1, 1, False)
                        with v.Fori(1, (DS - 1) // 2) as i:
                            make_hot(2 * i + 1, 1, True)
                            weigh(2 * i, 0, True)
                            make_hot(2 * i + 2, 0, True)
                            weigh(2 * i + 1, 1, True)
                        for s in range((DS - 1) // 2 * 2, DS):
                            if s + 1 < DS:
                                make_hot(s + 1, (s + 1) % 2, True)
                            weigh(s, s % 2, True)
                        v.wait_ge(placed, DS)
                        v.tensor_tensor(dinv[:], dinv[:], ps_degree[:, 0:NB], ALU.add)

                    @block.gpsimd
                    def _(pool):
                        def weigh(s, b, reuse):
                            pool.wait_ge(tallied, s + 1)
                            if reuse:
                                pool.wait_ge(placed, s - 1)
                            pool.sem_inc(weigh_open, 1)
                            for k in range(QS):
                                ins = pool.tensor_scalar(block_hot[:, b, k, :], iota_lo[0:CP, 0:NB],
                                                         step_block[:, b, k:k + 1], tally[:, b, k:k + 1],
                                                         ALU.is_equal, ALU.mult)
                            ins.then_inc(weighed, 1)

                        weigh(0, 0, False)
                        weigh(1, 1, False)
                        with pool.Fori(1, DS // 2) as i:
                            weigh(2 * i, 0, True)
                            weigh(2 * i + 1, 1, True)
                        if DS % 2:
                            weigh(DS - 1, 0, True)

                    if with_linear:
                        @block.scalar
                        def _(act):
                            link = chained(act, bn_step)
                            for c in range(CHUNKS + 2):
                                if c < CHUNKS:
                                    if c >= 2:
                                        act.wait_ge(h_turned, c - 1)
                                    for k in range(width(c)):
                                        n = c * BC + k
                                        ins = act.activation(h_ring[:, c % 2, k, :], xs[:, n, :], ACT.Relu,
                                                             scale=rstd[:, n:n + 1], bias=shift[:, n:n + 1])
                                    ins.then_inc(h_ready, 1)
                                if 1 <= c <= CHUNKS:
                                    n = width(c - 1) * P
                                    act.wait_ge(h_turned, c)
                                    if c >= 3:
                                        act.wait_ge(lin_ready, c - 2)
                                    act.copy(ht_ring[:, (c - 1) % 2, 0:n], ps_turn[(c - 1) % 2][:, 0:n])\
                                       .then_inc(ht_ready, 1)
                                if c >= 2:
                                    k = c - 2
                                    act.wait_ge(lin_ready, k + 1)
                                    act.activation(h_t[:, k * NC:min(N, (k + 1) * NC)],
                                                   ps_lin[k % 2][:, 0:min(N, (k + 1) * NC) - k * NC], ACT.Identity,
                                                   bias=B_GCN, accum_out=sums[:, 0, k:k + 1]).then_inc(lin_saved, 1)
                            act.wait_ge(lin_saved, CHUNKS)
                            link(act.activation(sums[:, 0, 0:CHUNKS], sums[:, 0, 0:CHUNKS], ACT.Identity,
                                                scale=-1.0 / N, accum_out=bn[:, 0:1]))
                            act.wait_ge(lin_ready, CHUNKS)
                            for k in range(CHUNKS):
                                ins = act.activation(ht_ring[:, 0, 0:min(N, (k + 1) * NC) - k * NC],
                                                     h_t[:, k * NC:min(N, (k + 1) * NC)], ACT.Square,
                                                     bias=bn[:, 0:1], accum_out=sums[:, 1, k:k + 1])
                                link(ins)
                            act.activation(sums[:, 1, 0:CHUNKS], sums[:, 1, 0:CHUNKS], ACT.Identity,
                                           scale=1.0 / N, accum_out=bn[:, 1:2])

                    @block.tensor
                    def _(pe):
                        def turn_h(c):
                            pe.wait_ge(h_ready, c + 1)
                            if c >= 2:
                                pe.wait_ge(ht_ready, c - 1)
                            for k in range(width(c)):
                                ins = pe.transpose(ps_turn[c % 2][:, k * P:(k + 1) * P], h_ring[:, c % 2, k, :],
                                                   ident[:])
                            ins.then_inc(h_turned, 1)

                        def apply_linear(c):
                            n = width(c) * P
                            pe.wait_ge(ht_ready, c + 1)
                            if c >= 2:
                                pe.wait_ge(lin_saved, c - 1)
                            pe.matmul(ps_lin[c % 2][:, 0:n], wg_t[:], ht_ring[:, c % 2, 0:n], start=True, stop=True)\
                              .then_inc(lin_ready, 1)

                        def count(s, b, reuse):
                            pe.wait_ge(hot_ready, s + 1)
                            if reuse:
                                pe.wait_ge(tallied, s - 1)
                            for k in range(QS):
                                for t in range(GT):
                                    windows = hot[b][:, t, k * CG:(k + 1) * CG, :].rearrange("p g n -> p (g n)")
                                    ins = pe.matmul(ps_tally[b][0:CP, k:k + 1], windows,
                                                    ones_col[:], start=(t == 0), stop=(t == GT - 1))
                            ins.then_inc(counted, 1)

                        def place(s, b, first=False, last=False):
                            pe.wait_ge(low_made, s + 1)
                            pe.wait_ge(weighed, s + 1)
                            for k in range(QS):
                                ins = pe.matmul(ps_degree[:, 0:NB], low_hot[:, b, k, :], block_hot[:, b, k, :],
                                                start=(first and k == 0), stop=(last and k == QS - 1))
                            ins.then_inc(placed, 1)

                        if with_linear:
                            for s in range(max(DS, -(-CHUNKS // 2)) + 1):
                                for c in (2 * s, 2 * s + 1):
                                    if c < CHUNKS:
                                        turn_h(c)
                                    if 1 <= c <= CHUNKS:
                                        apply_linear(c - 1)
                                if s < DS:
                                    count(s, s % 2, s >= 2)
                                if 1 <= s <= DS:
                                    place(s - 1, (s - 1) % 2, first=(s == 1), last=(s == DS))
                        else:
                            count(0, 0, False)
                            count(1, 1, False)
                            place(0, 0, first=True)
                            count(2, 0, True)
                            place(1, 1)
                            with pe.Fori(1, (DS - 1) // 2) as i:
                                count(2 * i + 1, 1, True)
                                place(2 * i, 0)
                                count(2 * i + 2, 0, True)
                                place(2 * i + 1, 1)
                            for s in range((DS - 1) // 2 * 2, DS):
                                if s + 1 < DS:
                                    count(s + 1, (s + 1) % 2, True)
                                place(s, s % 2, last=(s == DS - 1))

            degree_pass(True)
            with nc.If(passes > 1):
                with nc.Fori(1, passes):
                    degree_pass(False)
            with nc.Fori(0, passes):
                with nc.Block() as block:
                    @block.vector
                    def _(v):
                        v.tensor_scalar(rel[:], rel[:], float(W), None, ALU.add)

        with ExitStack() as scope:
            broot_ok, bn_link = (sem(n, scope) for n in ("broot_ok", "bn_link"))
            with nc.Block() as block:
                @block.scalar
                def _(act):
                    act.activation(bn[:, 2:3], bn[:, 1:2], ACT.Sqrt, bias=eps_col[:]).then_inc(broot_ok, 1)

                @block.vector
                def _(v):
                    link = chained(v, bn_link)
                    v.memset(h_t[:, N:], 0.0)
                    v.wait_ge(broot_ok, 1)
                    link(v.reciprocal(bn[:, 3:4], bn[:, 2:3]))
                    link(v.tensor_tensor(bn[:, 4:5], bn[:, 3:4], GAMMA, ALU.mult))
                    link(v.tensor_tensor(bn[:, 5:6], bn[:, 0:1], bn[:, 4:5], ALU.mult))
                    link(v.tensor_tensor(bn[:, 6:7], BETA, bn[:, 5:6], ALU.add))
                    v.tensor_scalar(h_t[:, 0:N], h_t[:, 0:N], bn[:, 4:5], bn[:, 6:7], ALU.mult, ALU.add)
        linear.close()

        with ExitStack() as scope:
            row_ring = sb("row_ring", [P, 2, BC, P], scope=scope)
            ps_rows = [bank(f"ps_rows{k}", [P, BC, P], scope) for k in range(2)]
            deg_root, dinv_ok, h_back, row_ready, high_ready, low_ready = (
                sem(n, scope) for n in ("deg_root", "dinv_ok", "h_back", "row_ready", "high_ready",
                                        "low_ready"))
            row_out = [sem(f"row_out{k}", scope) for k in range(2)]
            with nc.Block() as block:
                @block.gpsimd
                def _(pool):
                    pool.memset(acc[:], 0.0)

                @block.tensor
                def _(pe):
                    for c in range(CHUNKS):
                        if c >= 2:
                            pe.wait_ge(row_ready, c - 1)
                        for k in range(width(c)):
                            b = c * BC + k
                            ins = pe.transpose(ps_rows[c % 2][:, k, :], h_t[:, b * P:(b + 1) * P], ident[:])
                        ins.then_inc(h_back, 1)

                @block.scalar
                def _(act):
                    act.activation(dinv[:], dinv[:], ACT.Sqrt, bias=1.0).then_inc(deg_root, 1)
                    for c in range(CHUNKS):
                        n = width(c)
                        act.wait_ge(row_ready, c + 1)
                        act.copy(table_sb[:, c * BC:c * BC + n, 0, :], row_ring[:, c % 2, 0:n, :])\
                           .then_inc(high_ready, 1)

                @block.vector
                def _(v):
                    v.wait_ge(deg_root, 1)
                    v.reciprocal(dinv[:], dinv[:]).then_inc(dinv_ok, 1)
                    v.wait_ge(dinv_ok, 1)

                    def low_part(c):
                        n = width(c)
                        v.wait_ge(high_ready, c + 1)
                        v.tensor_tensor(table_sb[:, c * BC:c * BC + n, 1, :], row_ring[:, c % 2, 0:n, :],
                                        table_sb[:, c * BC:c * BC + n, 0, :].bitcast(F32), ALU.subtract)\
                         .then_inc(low_ready, 1)

                    for c in range(CHUNKS):
                        n = width(c)
                        if c >= 2:
                            v.wait_ge(row_out[c % 2], 16 * (c // 2))
                            v.wait_ge(low_ready, c - 1)
                        v.wait_ge(h_back, c + 1)
                        v.tensor_tensor(row_ring[:, c % 2, 0:n, :], ps_rows[c % 2][:, 0:n, :],
                                        dinv[:, c * BC:c * BC + n].unsqueeze(2).to_broadcast([P, n, P]), ALU.mult)\
                         .then_inc(row_ready, 1)
                        if c >= 1:
                            low_part(c - 1)
                    low_part(CHUNKS - 1)

                @block.sync
                def _(sp):
                    for c in range(CHUNKS):
                        n = width(c)
                        sp.wait_ge(row_ready, c + 1)
                        sp.dma_start(table_blocks[:, c * BC:c * BC + n, :], row_ring[:, c % 2, 0:n, :])\
                          .then_inc(row_out[c % 2], 16)
                    for k in range(2):
                        sp.wait_ge(row_out[k], 16 * ((CHUNKS - k + 1) // 2))

        early.close()

        PHASE = ["g", "e", "g", "e", "c", "e", "g", "e", "g", "e"]
        SLOTS = [0, 2, 4, 6, 8, 10, 12, 14, 15, 16]
        ITEMS = PHASE * DPI
        NI = len(ITEMS)
        AT = [CT * (j // len(PHASE)) + SLOTS[j % len(PHASE)] for j in range(NI)]
        LAG = 3
        ATTR = [j for j in range(NI) if ITEMS[j] != "c"]
        GATH = [j for j in range(NI) if ITEMS[j] == "g"]
        DENSE = [j for j in range(NI) if ITEMS[j] == "e"]
        CHNK = [j for j in range(NI) if ITEMS[j] == "c"]
        assert FULL + 1 <= GG + (STEPS - 1) * NG2
        LAST_ITEMS = [j for j in range(NI) if ITEMS[j] != "e"]
        PARTS = [b for b in range(3, CT)]
        BLOCKS_AT = {q: range(NB * k // len(PARTS), NB * (k + 1) // len(PARTS)) for k, q in enumerate(PARTS)}

        def start_of(j):
            return (GATH.index(j) if j in GATH else NG1 + DENSE.index(j) if j in DENSE else NGS + CHNK.index(j))

        def is_last(s):
            return isinstance(s, int) and s == STEPS - 1

        def buffer_of(j, s):
            return (LAST_ITEMS.index(j) if is_last(s) else j) % 2

        def group_of(j, s):
            return s * NG1 + GATH.index(j) if j in GATH else GG + s * NG2 + DENSE.index(j)

        with ExitStack() as scope:
            counts_sb = [sb(f"counts_sb{k}", [P, NB, CP], F32R, scope) for k in range(2)]
            lo_hot = sb("lo_hot", [P, HOTS, P], BF16, scope)
            key_hot = sb("key_hot", [P, HOTS, KEYS], BF16, scope)
            group_hots = sb("group_hots", [P, 2, GT, W], scope=scope)
            chunk_hot = sb("chunk_hot", [CP, WC], scope=scope)
            product = sb("product", [CP, 2, P], scope=scope)
            product_low = sb("product_low", [CP, 2, P], scope=scope)
            attr = sb("attr", [P, ATTRS, GT * P], scope=scope)
            gathered = sb("gathered", [P, GATHERS, GT, P], scope=scope)
            index = sb("index", [P, NG1, GT], I32, scope)
            ps_counts = [bank(f"ps_counts{k}", [P, 2, 512], scope) for k in range(2)]
            ps_product = [bank(f"ps_product{k}", [P, 512], scope) for k in range(2)]
            ps_sums = [bank(f"ps_sums{k}", [P, 512], scope) for k in range(2)]
            tile_moved, moved, hot_ready, built, saved, multiplied, low_saved, product_ready, index_ready, \
                item_hot, gathers_open = (
                sem(n, scope) for n in ("tile_moved", "moved", "hot_ready", "built", "saved", "multiplied",
                                        "low_saved", "product_ready", "index_ready", "item_hot",
                                        "gathers_open"))
            attr_in = [sem(f"attr_in{k}", scope) for k in range(ATTRS)]
            gather_in = [sem(f"gather_in{k}", scope) for k in range(NG1)]
            summed = [sem(f"summed{j}", scope) for j in range(NI)]
            added = [sem(f"added{j}", scope) for j in range(NI)]
            per_pass = (hot_ready, built, saved, multiplied, low_saved, product_ready, index_ready,
                        gathers_open,
                        item_hot, *attr_in, *gather_in)

            def need(eng, semaphore, count):
                if not isinstance(count, int) or count > 0:
                    eng.wait_ge(semaphore, count)

            def nth(j, s):
                return s if ITEMS[j] == "c" else s + 1

            def hots_until(j, s):
                if isinstance(s, int) and s == 0:
                    return j + 1 - ITEMS[:j].count("c")
                if is_last(s):
                    return s * NI - DPI + LAST_ITEMS.index(j) + 1
                return s * NI + j + 1 - DPI

            def loads_until(e, s):
                filled = sum(1 for i in range(e % ATTRS, e + 1, ATTRS) if not is_last(s) or ITEMS[ATTR[i]] == "g")
                return s * (NGS // ATTRS) + filled

            def before(j, k, s):
                if isinstance(s, int) and s == 0:
                    while j >= k and ITEMS[j - k] == "c":
                        k += k
                    return [(j - k, 1)] if j >= k else []
                if is_last(s):
                    n = LAST_ITEMS.index(j) - k
                    return [(LAST_ITEMS[n], nth(LAST_ITEMS[n], s)) if n >= 0 else (NI + n, nth(NI + n, s - 1))]
                i, t = (j - k, s) if j >= k else (j - k + NI, s - 1)
                return [(i, nth(i, t))]

            with nc.Fori(0, passes):
                with nc.Block() as block:
                    @block.vector
                    def _(v):
                        v.sem_clear(tile_moved)
                        link = chained(v, tile_moved)
                        v.tensor_scalar(drel[:], drel[:], -float(WT), None, ALU.add)
                        link(v.tensor_scalar(prel0[:], prel0[:], float(WT), None, ALU.add))
                        v.tensor_scalar(prel[:], prel0[:], float(WC), None, ALU.add)
                        starts_c = starts[:, 1:, NGS:NGS + DPI]
                        v.tensor_scalar(starts_c, chunk_start0[:].rearrange("a (s c) -> a s c", c=DPI), -float(WC),
                                        None, ALU.add)
                        link(v.tensor_scalar(inside[:], drel[:], 0.0, None, ALU.is_ge))
                        link(v.scalar_tensor_tensor(out=inside[:], in0=drel[:], scalar=float(WT), in1=inside[:],
                                                    op0=ALU.is_lt, op1=ALU.mult))
                        link(v.scalar_tensor_tensor(out=key[:], in0=drel[:], scalar=1.0, in1=inside[:],
                                                    op0=ALU.add, op1=ALU.mult))
                        link(v.tensor_tensor(inside[:], inside[:], src_hi[:], ALU.mult))
                        v.scalar_tensor_tensor(out=key[:], in0=key[:], scalar=-1.0, in1=inside[:],
                                               op0=ALU.add, op1=ALU.add)
                with nc.Fori(0, chunk_passes):
                    with nc.Block() as block:
                        @block.sync
                        def _(sp):
                            for s in summed:
                                sp.sem_clear(s)

                        @block.gpsimd
                        def _(pool):
                            for s in added:
                                pool.sem_clear(s)

                        @block.scalar
                        def _(act):
                            for s in per_pass:
                                act.sem_clear(s)

                        @block.vector
                        def _(v):
                            v.sem_clear(moved)
                            v.tensor_scalar(rel[:], rel[:], -float(W), None, ALU.add)
                            v.tensor_scalar(prel[:], prel[:], -float(WC), None, ALU.add)
                            v.tensor_scalar(starts[:, :, 0:NGS], starts[:, :, 0:NGS], float(W), None, ALU.add)
                            v.tensor_scalar(starts[:, 1:, NGS:NGS + DPI], starts[:, 1:, NGS:NGS + DPI], float(WC),
                                            None, ALU.add).then_inc(moved, 1)
                            v.wait_ge(moved, 1)
                            v.tensor_scalar(starts_int[:], starts[:], float(N), None, ALU.min)
                    with nc.Block() as block:
                        @block.sync
                        def _(sp):
                            def step(s):
                                for e, j in enumerate(ATTR):
                                    if is_last(s) and ITEMS[j] == "e":
                                        continue
                                    held = [i for i in range(e % ATTRS, e, ATTRS)
                                            if not is_last(s) or ITEMS[ATTR[i]] == "g"]
                                    if held:
                                        sp.wait_ge(summed[ATTR[held[-1]]], s + 1)
                                    else:
                                        need(sp, summed[ATTR[e % ATTRS - ATTRS]], s)
                                    g = group_of(j, s)
                                    if not isinstance(s, int):
                                        rows_of = attr_groups[bass.ds(g, 1), :, :].rearrange("a p n -> p (a n)")
                                    else:
                                        rows_of = attr_groups[g, :, :] if g < FULL else attr_last
                                    sp.dma_start(attr[:, e % ATTRS, :], rows_of).then_inc(attr_in[e % ATTRS], 16)
                            step(0)
                            whole_steps = (FULL - GG) // NG2
                            with sp.Fori(1, whole_steps) as s:
                                step(s)
                            for s in range(whole_steps, STEPS):
                                step(s)

                        @block.gpsimd
                        def _(pool):
                            def step(s):
                                for k in range(NG1):
                                    pool.wait_ge(index_ready, s * NG1 + k + 1)
                                    if k >= GATHERS:
                                        pool.wait_ge(summed[GATH[k - GATHERS]], s + 1)
                                    else:
                                        need(pool, summed[GATH[k - GATHERS]], s)
                                    pool.sem_inc(gathers_open, 1)
                                    for t in range(GT):
                                        pool.indirect_dma_start(
                                            gathered[:, k % GATHERS, t, :], None, table,
                                            bass.IndirectOffsetOnAxis(ap=index[:, k, t:t + 1], axis=0),
                                        ).then_inc(gather_in[k], 16)
                            step(0)
                            with pool.Fori(1, STEPS) as s:
                                step(s)

                        @block.scalar
                        def _(act):
                            def next_index(s, k):
                                need(act, gather_in[k], s * 16 * GT)
                                g = src_t[:, bass.ds(s * NG1 + k, 1), :].rearrange("p a t -> p (a t)")
                                act.copy(index[:, k, :], g).then_inc(index_ready, 1)

                            def save_product(s, phase):
                                need(act, multiplied, s * DPI + phase - 1)
                                need(act, summed[CHNK[phase]], s - 1)
                                act.copy(product_low[:, phase, :], ps_product[phase][0:CP, P:2 * P])\
                                   .then_inc(low_saved, 1)

                            def step(s):
                                for pair in range(DPI * CT // 2):
                                    phase, q = divmod(2 * pair, CT)
                                    act.wait_ge(built, s * DPI * CT + 2 * pair + 2)
                                    if q == 0:
                                        need(act, multiplied, s * DPI + phase - 1)
                                    act.copy(
                                        counts_sb[phase][:, :, q * WT:(q + 2) * WT].rearrange(
                                            "p h (t n) -> p t h n", n=WT),
                                        ps_counts[pair % 2][:, :, 0:KEYS].rearrange("p t (h n) -> p t h n", n=WT)
                                    ).then_inc(saved, 1)
                                    if q == 2 and not (isinstance(s, int) and s == 0):
                                        save_product(s, phase)
                                    for k, j in enumerate(GATH):
                                        if min(AT[j] // 2 + 1, DPI * CT // 2 - 1) == pair:
                                            next_index(s + 1, k)
                            for k in range(NG1):
                                next_index(0, k)
                            step(0)
                            step(1)
                            with act.Fori(2, STEPS - 1) as s:
                                step(s)
                            for phase in range(DPI):
                                save_product(STEPS - 1, phase)

                        @block.vector
                        def _(v):
                            regs = [v.alloc_register(f"start{k}") for k in range(NGS + DPI)]

                            def load_starts(s):
                                v.load(regs, starts_int[0:1, bass.ds(s, 1), 0:NGS + DPI].rearrange("a s g -> a (s g)"))

                            def chunk_item(s, j):
                                phase = CHNK.index(j)
                                v.wait_ge(low_saved, s * DPI + phase - 1)
                                v.tensor_tensor(product[:, phase, :], ps_product[phase][0:CP, 0:P],
                                                product_low[:, phase, :], ALU.add).then_inc(product_ready, 1)
                                prev = prel[:, bass.ds(s * DPI + CHNK.index(j) - DPI, 1)]
                                v.tensor_scalar(chunk_hot[:], iota_c[0:CP, :], prev, None, ALU.is_equal)\
                                 .then_inc(item_hot, 1)

                            def make_item(s, j):
                                for i, count in before(j, 2, s):
                                    v.wait_ge(summed[i], count)
                                if ITEMS[j] == "c":
                                    chunk_item(s, j)
                                else:
                                    group_hot(v, group_hots[:, buffer_of(j, s)], group_of(j, s), 1, iota_c[:, 0:W])\
                                        .then_inc(item_hot, 1)

                            def add_item(s, j, after):
                                for i, count in after:
                                    v.wait_ge(added[i], count)
                                v.wait_ge(summed[j], nth(j, s))
                                start = v.snap(regs[start_of(j)], min_val=0, max_val=N)
                                ps = ps_sums[buffer_of(j, s)]
                                if ITEMS[j] == "c":
                                    win, new = acc[:, 0, bass.ds(start, WC)], ps[:, 0:WC]
                                elif ITEMS[j] == "g":
                                    win = acc[:, :, bass.ds(start, W)]
                                    new = ps[:, 0:2 * W].rearrange("p (a n) -> p a n", a=2)
                                else:
                                    win, new = acc[:, 1, bass.ds(start, W)], ps[:, W:2 * W]
                                v.tensor_tensor(win, win, new, ALU.add).then_inc(added[j], 1)

                            def step(s):
                                zero = isinstance(s, int) and s == 0
                                load_starts(s)
                                for q in range(DPI * CT):
                                    need(v, built, s * DPI * CT + q + 1 - HOTS)
                                    tile = bass.ds(s * DPI * CT + q, 1)
                                    v.tensor_scalar(lo_hot[:, q % HOTS, :], iota_lo[:],
                                                    src_lo[:].rearrange("p g t -> p (g t)")[:, tile], None,
                                                    ALU.is_equal)
                                    v.tensor_scalar(key_hot[:, q % HOTS, :], iota_key[:],
                                                    key[:].rearrange("p g t -> p (g t)")[:, tile], None,
                                                    ALU.is_equal).then_inc(hot_ready, 1)
                                    if q in AT:
                                        j = AT.index(q)
                                        if not (zero and ITEMS[j] == "c"):
                                            make_item(s, j)
                                    if q - LAG in AT:
                                        j = AT.index(q - LAG)
                                        if not (zero and ITEMS[j] == "c"):
                                            add_item(s, j, before(j, 1, s))
                            step(0)
                            step(1)
                            with v.Fori(2, STEPS - 1) as s:
                                step(s)
                            last = STEPS - 1
                            load_starts(last)
                            for n, j in enumerate(LAST_ITEMS):
                                make_item(last, j)
                                if n >= 1:
                                    add_item(last, LAST_ITEMS[n - 1], before(LAST_ITEMS[n - 1], 1, last))
                            add_item(last, LAST_ITEMS[-1], before(LAST_ITEMS[-1], 1, last))

                        @block.tensor
                        def _(pe):
                            def multiply(s, phase, blocks):
                                b = 1 - phase
                                if blocks[0] == 0:
                                    pe.wait_ge(saved, (s * DPI + phase) * (CT // 2))
                                    need(pe, product_ready, s * DPI + phase - 2)
                                for h in blocks:
                                    ins = pe.matmul(ps_product[b][0:CP, 0:2 * P], counts_sb[b][:, h, :],
                                                    table_sb[:, h, :, :].rearrange("p a f -> p (a f)"),
                                                    start=(h == 0), stop=(h == NB - 1))
                                if blocks[-1] == NB - 1:
                                    ins.then_inc(multiplied, 1)

                            def sum_chunk(s, j):
                                phase = CHNK.index(j)
                                pe.wait_ge(product_ready, s * DPI + phase - 1)
                                pe.wait_ge(item_hot, hots_until(j, s))
                                pe.matmul(ps_sums[buffer_of(j, s)][:, 0:WC], product[:, phase, :], chunk_hot[:],
                                          start=True, stop=True).then_inc(summed[j], 1)

                            def sum_group(s, j):
                                e = ATTR.index(j)
                                ps = ps_sums[buffer_of(j, s)]
                                pe.wait_ge(item_hot, hots_until(j, s))
                                pe.wait_ge(attr_in[e % ATTRS], 16 * loads_until(e, s))
                                for t in range(GT):
                                    ins = pe.matmul(ps[:, W:2 * W], attr[:, e % ATTRS, t * P:(t + 1) * P],
                                                    group_hots[:, buffer_of(j, s), t, :], start=(t == 0),
                                                    stop=(t == GT - 1))
                                if j in GATH:
                                    k = GATH.index(j)
                                    pe.wait_ge(gather_in[k], 16 * GT * (s + 1))
                                    for t in range(GT):
                                        ins = pe.matmul(ps[:, 0:W], gathered[:, k % GATHERS, t, :],
                                                        group_hots[:, buffer_of(j, s), t, :],
                                                        start=(t == 0), stop=(t == GT - 1))
                                ins.then_inc(summed[j], 1)

                            def sum_item(s, j):
                                for i, count in before(j, 2, s):
                                    pe.wait_ge(added[i], count)
                                if ITEMS[j] == "c":
                                    sum_chunk(s, j)
                                else:
                                    sum_group(s, j)

                            def step(s):
                                zero = isinstance(s, int) and s == 0
                                for q in range(DPI * CT):
                                    phase, slot = divmod(q, CT)
                                    if q % 2 == 0:
                                        need(pe, saved, s * (DPI * CT // 2) + q // 2 - 1)
                                    pe.wait_ge(hot_ready, s * DPI * CT + q + 1)
                                    pe.matmul(ps_counts[q // 2 % 2][:, q % 2, 0:KEYS], lo_hot[:, q % HOTS, :],
                                              key_hot[:, q % HOTS, :], start=True, stop=True).then_inc(built, 1)
                                    if slot in BLOCKS_AT and not (zero and phase == 0):
                                        multiply(s, phase, BLOCKS_AT[slot])
                                    if q in AT:
                                        j = AT.index(q)
                                        if zero and ITEMS[j] == "c":
                                            continue
                                        sum_item(s, j)
                            step(0)
                            step(1)
                            with pe.Fori(2, STEPS - 1) as s:
                                step(s)
                            for n, j in enumerate(LAST_ITEMS):
                                sum_item(STEPS - 1, j)
                                if n == 0:
                                    multiply(STEPS - 1, 0, range(NB))

        with ExitStack() as scope:
            def ring(name):
                return sb(name, [P, 2, NC], scope=scope)

            xs = sb("xs2", [P, NB, P], scope=scope)
            stats = sb("stats2", [P, NB, 6], scope=scope)
            self_ring, conv_ring, relu_ring, h2_ring, h2t_ring, z1_ring, z2_ring, y_ring = (
                ring(n) for n in ("self_ring", "conv_ring", "relu_ring", "h2_ring", "h2t_ring", "z1_ring", "z2_ring",
                                  "y_ring"))
            ps_turn, ps_1, ps_2, ps_3 = ([bank(f"ps_{n}{k}", [P, NC], scope) for k in range(2)]
                                         for n in ("t", "one", "two", "three"))
            (zeroed, self_ready, conv_turned, conv_ready, relu_ready, x1_ready, var_ok, root_ok, norm_ok, dve_step,
             h2_ready, h2_turned, h2t_ready, m1_ready, z1_ready, m2_ready, z2_ready, m3_ready, y_ready) = (
                sem(f"mlp_{n}", scope) for n in
                "zeroed self_ready conv_turned conv_ready relu_ready x1_ready var_ok root_ok norm_ok dve_step "
                "h2_ready h2_turned h2t_ready m1_ready z1_ready m2_ready z2_ready m3_ready y_ready".split())
            x_in = [sem(f"mlp_x_in{c}", scope) for c in range(CHUNKS)]
            y_out = [sem(f"y_out{k}", scope) for k in range(2)]

            b3_rows = sb("b3_rows", [P, P], scope=scope)
            sum_ring, x3_ring = ring("sum_ring"), ring("x3_ring")
            b3_in, agg_ready, agg_saved, sum_ready, x3_ready = (
                sem(f"mlp_{n}", scope) for n in "b3_in agg_ready agg_saved sum_ready x3_ready".split())

            def chunk(rows_of, c):
                return rows_of[:, c * BC:c * BC + width(c), :].rearrange("p b f -> p (b f)")

            def slot(buffers, c):
                return buffers[:, c % 2, 0:width(c) * P]

            M1_AT, SUM_AT, Z1_AT, M2_AT, Z2_AT, M3_AT, Y_AT = 1, 2, 2, 3, 4, 5, 6

            with nc.Block() as block:
                @block.sync
                def _(sp):
                    for c in range(CHUNKS - 1):
                        sp.dma_start(xs[:, c * BC:(c + 1) * BC, :], x_full[:, c * BC:(c + 1) * BC, :])\
                          .then_inc(x_in[c], 16)
                    sp.wait_ge(zeroed, 1)
                    sp.dma_start(xs[0:TAILN, FB, :], x[FB * P:N, :]).then_inc(x_in[CHUNKS - 1], 16)
                    sp.dma_start(b3_rows[:], b3.rearrange("(a n) -> a n", a=1).to_broadcast([P, P]))\
                      .then_inc(b3_in, 16)
                    for c in range(CHUNKS):
                        sp.wait_ge(y_ready, c + 1)
                        rows_of = y_ring[:, c % 2, :].rearrange("p (b f) -> p b f", b=BC)
                        if c < CHUNKS - 1:
                            sp.dma_start(out_full[:, c * BC:(c + 1) * BC, :], rows_of).then_inc(y_out[c % 2], 16)
                        else:
                            sp.dma_start(out[FB * P:N, :], rows_of[0:TAILN, 0, :]).then_inc(y_out[c % 2], 16)
                    for k in range(2):
                        sp.wait_ge(y_out[k], 16 * ((CHUNKS - k + 1) // 2))

                @block.gpsimd
                def _(pool):
                    pool.memset(xs[:, FB, :], 0.0).then_inc(zeroed, 1)
                    for c in range(CHUNKS):
                        n = width(c)
                        if c >= 2:
                            pool.wait_ge(conv_ready, c - 1)
                        parts = table_sb[:, c * BC:c * BC + n, :, :].bitcast(F32)
                        pool.tensor_tensor(slot(self_ring, c).rearrange("p (b f) -> p b f", b=n), parts[:, :, 0, :],
                                           parts[:, :, 1, :], ALU.add).then_inc(self_ready, 1)
                    pool.wait_ge(b3_in, 16)
                    pool.wait_ge(x1_ready, CHUNKS)
                    for c in range(CHUNKS):
                        n = width(c)
                        if c >= 2:
                            pool.wait_ge(y_ready, c - 1)
                        pool.tensor_tensor(slot(x3_ring, c).rearrange("p (b f) -> p b f", b=n),
                                           xs[:, c * BC:c * BC + n, :],
                                           b3_rows[:].unsqueeze(1).to_broadcast([P, n, P]), ALU.add)\
                            .then_inc(x3_ready, 1)

                @block.vector
                def _(v):
                    link = chained(v, dve_step)

                    def add_conv(c):
                        v.wait_ge(x_in[c], 16)
                        v.wait_ge(relu_ready, c + 1)
                        v.tensor_tensor(chunk(xs, c), slot(relu_ring, c), chunk(xs, c), ALU.add).then_inc(x1_ready, 1)
                        v.wait_ge(x1_ready, c + 1)
                        for b in range(c * BC, c * BC + width(c)):
                            ins = v.bn_stats(stats[:, b, :], xs[:, b, :])
                        return ins

                    for c in range(CHUNKS):
                        v.wait_ge(self_ready, c + 1)
                        v.wait_ge(conv_turned, c + 1)
                        if c >= 2:
                            v.wait_ge(relu_ready, c - 1)
                        v.tensor_tensor(slot(conv_ring, c), ps_turn[c % 2][:, 0:width(c) * P], slot(self_ring, c),
                                        ALU.add).then_inc(conv_ready, 1)
                        if c >= 1:
                            add_conv(c - 1)
                    link(add_conv(CHUNKS - 1))
                    layer_norm_stats(v, link, stats, var_ok, root_ok, norm_ok)

                    for s in range(CHUNKS + Y_AT):
                        if SUM_AT <= s < CHUNKS + SUM_AT:
                            c = s - SUM_AT
                            v.wait_ge(m1_ready, c + 1)
                            v.wait_ge(agg_saved, CHUNKS)
                            if c >= 2:
                                v.wait_ge(z1_ready, c - 1)
                            v.tensor_tensor(slot(sum_ring, c), ps_1[c % 2][:, 0:width(c) * P],
                                            acc[:, 1, c * NC:c * NC + width(c) * P], ALU.add).then_inc(sum_ready, 1)
                        if s < CHUNKS:
                            v.wait_ge(h2_turned, s + 1)
                            if s >= 2:
                                v.wait_ge(m1_ready, s - 1)
                            v.tensor_copy(slot(h2t_ring, s), ps_turn[s % 2][:, 0:width(s) * P]).then_inc(h2t_ready, 1)
                        if s >= Y_AT:
                            c = s - Y_AT
                            v.wait_ge(m3_ready, c + 1)
                            v.wait_ge(x3_ready, c + 1)
                            if c >= 2:
                                v.wait_ge(y_out[c % 2], 16 * (c // 2))
                            v.tensor_tensor(slot(y_ring, c), ps_3[c % 2][:, 0:width(c) * P], slot(x3_ring, c), ALU.add)\
                             .then_inc(y_ready, 1)

                @block.scalar
                def _(act):
                    for c in range(CHUNKS):
                        act.wait_ge(conv_ready, c + 1)
                        if c >= 2:
                            act.wait_ge(x1_ready, c - 1)
                        for k in range(width(c)):
                            b = c * BC + k
                            part = slice(k * P, (k + 1) * P)
                            ins = act.activation(relu_ring[:, c % 2, part], conv_ring[:, c % 2, part], ACT.Relu,
                                                 scale=dinv[:, b:b + 1])
                        ins.then_inc(relu_ready, 1)
                        act.wait_ge(agg_ready, c + 1)
                        n = width(c) * P
                        act.copy(acc[:, 1, c * NC:c * NC + n], ps_2[c % 2][:, 0:n]).then_inc(agg_saved, 1)
                    act.wait_ge(var_ok, 1)
                    act.activation(rstd[:], var[:], ACT.Sqrt, bias=eps_col[:]).then_inc(root_ok, 1)
                    act.wait_ge(norm_ok, 1)
                    for s in range(CHUNKS + Z2_AT):
                        if s < CHUNKS:
                            if s >= 2:
                                act.wait_ge(h2_turned, s - 1)
                            for k in range(width(s)):
                                n = s * BC + k
                                ins = act.activation(h2_ring[:, s % 2, k * P:(k + 1) * P], xs[:, n, :], ACT.Relu,
                                                     scale=rstd[:, n:n + 1], bias=shift[:, n:n + 1])
                            ins.then_inc(h2_ready, 1)
                        if Z1_AT <= s < CHUNKS + Z1_AT:
                            c = s - Z1_AT
                            act.wait_ge(sum_ready, c + 1)
                            if c >= 2:
                                act.wait_ge(m2_ready, c - 1)
                            act.activation(slot(z1_ring, c), slot(sum_ring, c), ACT.Relu, bias=b1u[:])\
                               .then_inc(z1_ready, 1)
                        if s >= Z2_AT:
                            c = s - Z2_AT
                            act.wait_ge(m2_ready, c + 1)
                            if c >= 2:
                                act.wait_ge(m3_ready, c - 1)
                            act.activation(slot(z2_ring, c), ps_2[c % 2][:, 0:width(c) * P], ACT.Relu, bias=B2)\
                               .then_inc(z2_ready, 1)

                @block.tensor
                def _(pe):
                    for c in range(CHUNKS):
                        if c >= 2:
                            pe.wait_ge(conv_ready, c - 1)
                        for k in range(width(c)):
                            b = c * BC + k
                            ins = pe.transpose(ps_turn[c % 2][:, k * P:(k + 1) * P], acc[:, 0, b * P:(b + 1) * P],
                                               ident[:])
                        ins.then_inc(conv_turned, 1)
                        n = width(c) * P
                        if c >= 2:
                            pe.wait_ge(agg_saved, c - 1)
                        pe.matmul(ps_2[c % 2][:, 0:n], w1_sb[:, 1, :], acc[:, 1, c * NC:c * NC + n], start=True,
                                  stop=True).then_inc(agg_ready, 1)
                    pe.wait_ge(conv_ready, CHUNKS)
                    pe.wait_ge(agg_saved, CHUNKS)
                    for s in range(CHUNKS + M3_AT):
                        if s < CHUNKS:
                            pe.wait_ge(h2_ready, s + 1)
                            if s >= 2:
                                pe.wait_ge(h2t_ready, s - 1)
                            for k in range(width(s)):
                                part = slice(k * P, (k + 1) * P)
                                ins = pe.transpose(ps_turn[s % 2][:, part], h2_ring[:, s % 2, part], ident[:])
                            ins.then_inc(h2_turned, 1)
                        if M1_AT <= s < CHUNKS + M1_AT:
                            c = s - M1_AT
                            n = width(c) * P
                            pe.wait_ge(h2t_ready, c + 1)
                            if c >= 2:
                                pe.wait_ge(sum_ready, c - 1)
                            pe.matmul(ps_1[c % 2][:, 0:n], w1_sb[:, 0, :], slot(h2t_ring, c), start=True, stop=True)\
                              .then_inc(m1_ready, 1)
                        if M2_AT <= s < CHUNKS + M2_AT:
                            c = s - M2_AT
                            pe.wait_ge(z1_ready, c + 1)
                            if c >= 2:
                                pe.wait_ge(z2_ready, c - 1)
                            pe.matmul(ps_2[c % 2][:, 0:width(c) * P], w2_sb[:], slot(z1_ring, c), start=True,
                                      stop=True).then_inc(m2_ready, 1)
                        if s >= M3_AT:
                            c = s - M3_AT
                            pe.wait_ge(z2_ready, c + 1)
                            if c >= 2:
                                pe.wait_ge(y_ready, c - 1)
                            for k in range(width(c)):
                                part = slice(k * P, (k + 1) * P)
                                ins = pe.matmul(ps_3[c % 2][:, part], z2_ring[:, c % 2, part], w3_sb[:], start=True,
                                                stop=True)
                            ins.then_inc(m3_ready, 1)


_INS = ['x', 'src', 'dst', 'edge_attr_128', 'L0_gnn_W', 'L0_gnn_b', 'L0_gnn_gamma', 'L0_gnn_beta', 'L1_gnn_u',
        'L1_gnn_W1', 'L1_gnn_b1', 'L1_gnn_W2', 'L1_gnn_b2', 'L1_gnn_W3', 'L1_gnn_b3']
_OUTS = [((6250, 128), 'float32')]


def kernel(**inputs):
    import numpy as _np
    import concourse.bacc as _bacc
    from concourse import mybir as _mybir
    from concourse.bass_utils import run_bass_kernel_spmd as _run

    nc = _bacc.Bacc("TRN2", target_bir_lowering=False, num_devices=1)
    arrays, args = {}, []
    for name in _INS:
        a = _np.ascontiguousarray(inputs[name])
        arrays[f"in_{name}_dram"] = a
        args.append(nc.dram_tensor(f"in_{name}_dram", a.shape, _mybir.dt.from_np(a.dtype), kind="ExternalInput").ap())
    for i, (shape, dtype) in enumerate(_OUTS):
        dt = _mybir.dt.from_np(_np.dtype(dtype))
        args.append(nc.dram_tensor(f"out_{i}_dram", shape, dt, kind="ExternalOutput").ap())
    gnn_kernel(nc, *args)
    r = _run(nc, [arrays], core_ids=[0])
    got = tuple(r.results[0][f"out_{i}_dram"] for i in range(len(_OUTS)))
    return got[0]
```
